# Optimizing a Trainium2 kernel written in Bass

```python
import numpy as np
import jax
import jax.numpy as jnp

def _softmax(x, axis=-1):
    return jax.nn.softmax(x, axis=axis)

def _gelu(x):
    return jax.nn.gelu(x, approximate=True)

def _silu(x):
    return jax.nn.silu(x)

def _sigmoid(x):
    return jax.nn.sigmoid(x)

def _layernorm(x, axis=-1, eps=1e-05):
    m = jnp.mean(x, axis=axis, keepdims=True)
    v = jnp.var(x, axis=axis, keepdims=True)
    return (x - m) / jnp.sqrt(v + eps)

def _scatter_add(tgt, idx, src, axis=0):
    return tgt.at[idx].add(src)

def _segment_sum(src, seg, n):
    return jax.ops.segment_sum(src, seg, n)
kernel_name = 'mk_seq_postln_d1_jaxref_r8_6560d0'

def setup_inputs(seed: int=0):
    np.random.seed(seed)
    _w = jnp.asarray

    def _L0_attn_setup():
        import jax, jax.numpy as jnp
        import numpy as np
        D_MODEL = 128
        D_STATE = 128
        D_CONV = 4
        EXPAND = 2
        HEADDIM = 64
        D_INNER = EXPAND * D_MODEL
        NHEADS = D_INNER // HEADDIM
        CONV_DIM = D_INNER + 2 * D_STATE
        D_IN_PROJ = 2 * D_INNER + 2 * D_STATE + NHEADS
        EPS = 1e-05
        B, L = (2, 512)
        key = jax.random.key(seed)
        ks = jax.random.split(key, 8)
        return {'x': jax.random.normal(ks[0], (B, L, D_MODEL), dtype=jnp.float32), 'in_proj_w': jax.random.normal(ks[1], (D_MODEL, D_IN_PROJ), dtype=jnp.float32) * 0.02, 'conv_w': jax.random.normal(ks[2], (D_CONV, CONV_DIM), dtype=jnp.float32) * 0.2, 'conv_b': jnp.zeros((CONV_DIM,), dtype=jnp.float32), 'norm_w': jnp.ones((D_INNER,), dtype=jnp.float32), 'out_proj_w': jax.random.normal(ks[3], (D_INNER, D_MODEL), dtype=jnp.float32) * 0.02, 'dt_bias': jax.random.normal(ks[4], (NHEADS,), dtype=jnp.float32) * 0.1, 'A_log': jax.random.normal(ks[5], (NHEADS,), dtype=jnp.float32) * 0.1, 'D': jnp.ones((NHEADS,), dtype=jnp.float32)}
    _L0_attn_in = _L0_attn_setup()

    def _L0_ffn_setup():
        import jax, jax.numpy as jnp
        import numpy as np
        D_MODEL = 128
        HIDDEN = 256
        E_ROUTED = 14
        E_SHARED = 2
        TOP_K = 2
        EPS = 1e-09
        RMS_EPS = 1.1920929e-07

        def _ffn(xn, rw, W1, W2):
            ms = jnp.mean(xn * xn, axis=-1, keepdims=True)
            h = xn * jax.lax.rsqrt(ms + RMS_EPS) * rw
            return jax.nn.silu(h @ W1) @ W2
        key = jax.random.key(seed)
        ks = jax.random.split(key, 9)
        B, T = (2, 128)
        x = jax.random.normal(ks[0], (B, T, D_MODEL), dtype=jnp.float32)
        router_w = jax.random.normal(ks[1], (D_MODEL, E_ROUTED), dtype=jnp.float32) * 0.006
        rms_w = jnp.ones((E_ROUTED, D_MODEL), dtype=jnp.float32)
        w1 = jax.random.normal(ks[2], (E_ROUTED, D_MODEL, HIDDEN), dtype=jnp.float32) * 0.02
        w2 = jax.random.normal(ks[3], (E_ROUTED, HIDDEN, D_MODEL), dtype=jnp.float32) * 0.02
        rms_w_s = jnp.ones((E_SHARED, D_MODEL), dtype=jnp.float32)
        w1_s = jax.random.normal(ks[4], (E_SHARED, D_MODEL, HIDDEN), dtype=jnp.float32) * 0.02
        w2_s = jax.random.normal(ks[5], (E_SHARED, HIDDEN, D_MODEL), dtype=jnp.float32) * 0.02
        return {'x': x, 'router_w': router_w, 'rms_w': rms_w, 'w1': w1, 'w2': w2, 'rms_w_s': rms_w_s, 'w1_s': w1_s, 'w2_s': w2_s}
    _L0_ffn_in = _L0_ffn_setup()
    _d = {'L0_attn_x': _L0_attn_in['x'], 'L0_attn_in_proj_w': _L0_attn_in['in_proj_w'], 'L0_attn_conv_w': _L0_attn_in['conv_w'], 'L0_attn_conv_b': _L0_attn_in['conv_b'], 'L0_attn_norm_w': _L0_attn_in['norm_w'], 'L0_attn_out_proj_w': _L0_attn_in['out_proj_w'], 'L0_attn_dt_bias': _L0_attn_in['dt_bias'], 'L0_attn_A_log': _L0_attn_in['A_log'], 'L0_attn_D': _L0_attn_in['D'], 'L0_ffn_router_w': _L0_ffn_in['router_w'], 'L0_ffn_rms_w': _L0_ffn_in['rms_w'], 'L0_ffn_w1': _L0_ffn_in['w1'], 'L0_ffn_w2': _L0_ffn_in['w2'], 'L0_ffn_rms_w_s': _L0_ffn_in['rms_w_s'], 'L0_ffn_w1_s': _L0_ffn_in['w1_s'], 'L0_ffn_w2_s': _L0_ffn_in['w2_s']}
    _x0 = _d['L0_attn_x']
    _d['L0_attn_x'] = jax.random.normal(jax.random.fold_in(jax.random.key(seed), 1), (8, 1024, 128), dtype=_x0.dtype)
    del _x0
    return _d

def reference(L0_attn_x, L0_attn_in_proj_w, L0_attn_conv_w, L0_attn_conv_b, L0_attn_norm_w, L0_attn_out_proj_w, L0_attn_dt_bias, L0_attn_A_log, L0_attn_D, L0_ffn_router_w, L0_ffn_rms_w, L0_ffn_w1, L0_ffn_w2, L0_ffn_rms_w_s, L0_ffn_w1_s, L0_ffn_w2_s):

    def _L0_attn_ref(x, in_proj_w, conv_w, conv_b, norm_w, out_proj_w, dt_bias, A_log, D):
        import jax, jax.numpy as jnp
        import numpy as np
        D_MODEL = 128
        D_STATE = 128
        D_CONV = 4
        EXPAND = 2
        HEADDIM = 64
        D_INNER = EXPAND * D_MODEL
        NHEADS = D_INNER // HEADDIM
        CONV_DIM = D_INNER + 2 * D_STATE
        D_IN_PROJ = 2 * D_INNER + 2 * D_STATE + NHEADS
        EPS = 1e-05
        B, L = (2, 512)
        Bb, Ll, _ = x.shape
        zxbcdt = jnp.einsum('bld,df->blf', x, in_proj_w)
        z, xBC, dt = jnp.split(zxbcdt, [D_INNER, D_INNER + CONV_DIM], axis=-1)
        xp = jnp.pad(xBC, ((0, 0), (D_CONV - 1, 0), (0, 0)))
        y_conv = conv_b
        for k in range(D_CONV):
            y_conv = y_conv + xp[:, k:k + Ll, :] * conv_w[D_CONV - 1 - k]
        xBC = jax.nn.silu(y_conv)
        x_part, B_part, C_part = jnp.split(xBC, [D_INNER, D_INNER + D_STATE], axis=-1)
        x_heads = x_part.reshape(Bb, Ll, NHEADS, HEADDIM)
        dt = jax.nn.softplus(dt + dt_bias)
        A = -jnp.exp(A_log)
        state0 = jnp.zeros((Bb, NHEADS, HEADDIM, D_STATE), dtype=x.dtype)

        def scan_fn(state, inp):
            dt_t, x_t, B_t, C_t = inp
            decay = jnp.exp(A[None, :] * dt_t)
            state = state * decay[:, :, None, None]
            state = state + (x_t * dt_t[:, :, None])[..., None] * B_t[:, None, None, :]
            y_t = jnp.einsum('bhpn,bn->bhp', state, C_t)
            return (state, y_t)
        _, y_acc = jax.lax.scan(scan_fn, state0, (dt.transpose(1, 0, 2), x_heads.transpose(1, 0, 2, 3), B_part.transpose(1, 0, 2), C_part.transpose(1, 0, 2)))
        y = y_acc.transpose(1, 0, 2, 3).reshape(Bb, Ll, D_INNER)
        y = y + x_part * jnp.repeat(D, HEADDIM)[None, None, :]
        g = y * jax.nn.silu(z)
        g = g * jax.lax.rsqrt(jnp.mean(g ** 2, axis=-1, keepdims=True) + EPS) * norm_w
        return jnp.einsum('bld,df->blf', g, out_proj_w)

    def _L0_ffn_ref(x, router_w, rms_w, w1, w2, rms_w_s, w1_s, w2_s):
        import jax, jax.numpy as jnp
        import numpy as np
        D_MODEL = 128
        HIDDEN = 256
        E_ROUTED = 14
        E_SHARED = 2
        TOP_K = 2
        EPS = 1e-09
        RMS_EPS = 1.1920929e-07

        def _ffn(xn, rw, W1, W2):
            ms = jnp.mean(xn * xn, axis=-1, keepdims=True)
            h = xn * jax.lax.rsqrt(ms + RMS_EPS) * rw
            return jax.nn.silu(h @ W1) @ W2
        B, T, D = x.shape
        N = B * T
        xf = x.reshape(N, D)
        gates = jax.nn.softmax(xf @ router_w, axis=-1)
        top_v, top_i = jax.lax.top_k(gates, TOP_K)
        masked = jnp.zeros_like(gates).at[jnp.arange(N)[:, None], top_i].set(top_v)
        masked = masked / (masked.sum(axis=-1, keepdims=True) + EPS)
        routed = jax.vmap(lambda rw_, W1_, W2_: _ffn(xf, rw_, W1_, W2_))(rms_w, w1, w2)
        routed_out = jnp.einsum('end,ne->nd', routed, masked)
        shared = jax.vmap(lambda rw_, W1_, W2_: _ffn(xf, rw_, W1_, W2_))(rms_w_s, w1_s, w2_s).sum(0)
        return (routed_out + shared).reshape(B, T, D)
    x = L0_attn_x
    x = _layernorm(x + _L0_attn_ref(x, L0_attn_in_proj_w, L0_attn_conv_w, L0_attn_conv_b, L0_attn_norm_w, L0_attn_out_proj_w, L0_attn_dt_bias, L0_attn_A_log, L0_attn_D), axis=-1)
    x = _layernorm(x + _L0_ffn_ref(x, L0_ffn_router_w, L0_ffn_rms_w, L0_ffn_w1, L0_ffn_w2, L0_ffn_rms_w_s, L0_ffn_w1_s, L0_ffn_w2_s), axis=-1)
    return x

_drawn_inputs = setup_inputs


def setup_inputs(seed=0):
    import zlib

    import numpy as np

    out = dict(_drawn_inputs(seed))
    spreads = {'L0_attn_conv_b': (0.0, 0.1),
     'L0_attn_norm_w': (1.0, 0.2),
     'L0_attn_D': (1.0, 0.595),
     'L0_ffn_rms_w': (1.0, 0.6),
     'L0_ffn_rms_w_s': (1.0, 0.6)}
    factors = {'L0_attn_dt_bias': 64.0, 'L0_attn_A_log': 200.0}
    for name, (base, spread) in spreads.items():
        noise = np.random.default_rng([zlib.crc32(name.encode()), seed]).standard_normal(out[name].shape)
        drawn = base * np.exp(spread * noise) if base else spread * noise
        out[name] = jnp.asarray(drawn.astype(out[name].dtype))
    for name, factor in factors.items():
        out[name] = (out[name] * factor).astype(out[name].dtype)
    return out
```

```python
from contextlib import ExitStack

import concourse.bass as bass
from concourse import mybir

F32 = mybir.dt.float32
U32 = mybir.dt.uint32
ALU = mybir.AluOpType
ACT = mybir.ActivationFunctionType
AX = mybir.AxisListType
P = 128
BANK = 512
TAPS = 4
TOP_K = 2
LN_EPS = 1e-5
RMS_EPS = 1.1920929e-07
GATE_EPS = 1e-9
A_FLOOR = -200.0
LOG1P_TERMS = 8


class Queue:

    def __init__(self, name, counts):
        self.name, self.steps, self.seen, self.counts = name, [], {}, counts

    def put(self, make, after=(), signal=None, by=1):
        waits = []
        for done in after:
            if done is not None and self.seen.get(done[0], 0) < done[1]:
                self.seen[done[0]] = done[1]
                waits.append(done)
        token = None
        if signal is not None:
            self.counts[signal] = self.counts.get(signal, 0) + by
            token = (signal, self.counts[signal])
        self.steps.append((waits, make, signal, by))
        return token

    def play(self, engine, semaphores):
        for waits, make, signal, by in self.steps:
            for name, value in waits:
                engine.wait_ge(semaphores[name], value)
            made = make(engine)
            if signal is not None:
                made.then_inc(semaphores[signal], by)


class Ring:

    def __init__(self, buffers):
        self.buffers, self.free, self.at = buffers, [()] * len(buffers), -1

    def take(self):
        self.at = (self.at + 1) % len(self.buffers)
        return self.at, self.buffers[self.at], self.free[self.at]


def mamba_moe(nc, xT_d, x_d, w_in_d, conv_w_d, conv_b_d, norm_w_d, w_out_d, dt_bias_d, a_log_d,
              d_skip_d, router_d, rms_w_d, w1_d, w2_d, out_d):
    D = xT_d.shape[0]
    TOK = xT_d.shape[1]
    NB = 8
    NC = TOK // P
    CPB = NC // NB
    NT = NC // 4
    TPB = NT // NB
    NH = dt_bias_d.shape[1]
    DI = norm_w_d.shape[1] * P
    HD = DI // NH
    NBLK = conv_b_d.shape[1]
    NE = w1_d.shape[1] // (2 * P)
    NR = router_d.shape[1]
    HB = 2
    W = 4 * P

    counts = {}
    pe, act, dve, pool, sp = (Queue(n, counts) for n in ("pe", "act", "dve", "pool", "sp"))

    with ExitStack() as ctx:
        def sb(name, shape, dt=F32):
            return ctx.enter_context(nc.sbuf_tensor(name, shape, dt))

        xT = sb("xT", [P, TOK])
        x = sb("x", [P, NC, D])
        w_in = sb("w_in", [P, w_in_d.shape[1]])
        conv_w = sb("conv_w", [P, NBLK, TAPS])
        conv_b = sb("conv_b", [P, NBLK])
        norm_w = sb("norm_w", [P, DI // P])
        w_out = sb("w_out", [P, DI // P, D])
        dt_bias = sb("dt_bias", [P, NH])
        a_log = sb("a_log", [P, NH])
        d_skip = sb("d_skip", [P, NH])
        router = sb("router", [P, NR])
        rms_w = sb("rms_w", [P, NE])
        w1_shared = sb("w1_shared", [P, NE - NR, HB * P])
        w2_shared = sb("w2_shared", [P, NE - NR, HB, D])
        ident = sb("ident", [P, P])
        upto = sb("upto", [P, P])
        beyond = sb("beyond", [P, P])
        ones = sb("ones", [P, P])
        neg_half = sb("neg_half", [P, 8])
        half = sb("half", [P, 8])
        expert_no = sb("expert_no", [P, NR])
        expert_no_i = sb("expert_no_i", [P, NR], mybir.dt.int32)
        a_rate = sb("a_rate", [P, NH])
        dt_raw = sb("dt_raw", [P, NC, NH])
        dt_s = sb("dt_s", [P, NC, NH])
        dt_p = sb("dt_p", [P, NC, NH])
        dt_q = sb("dt_q", [P, NC, NH])
        dt = sb("dt", [P, NC, NH])
        a_log_step = sb("a_log_step", [P, NC, NH])
        into = sb("into", [P, NC, NH])
        outof = sb("outof", [P, NC, NH])
        whole = sb("whole", [P, NC, NH])
        arow = [sb(f"arow{i}", [P, NH, P]) for i in range(2)]
        decay_area = sb("decay_area", [P, CPB + 3, NH, P])
        decay = [decay_area[:, i] for i in range(CPB + 3)]
        w1_routed = decay_area[:].rearrange("p n h i -> p (n h i)")[:, 0:NR * HB * P].rearrange("p (e f) -> p e f", e=NR)
        raw_area = sb("raw_area", [P, 2, NBLK, TAPS - 1 + W])
        raw = [raw_area[:, i] for i in range(2)]
        w2_routed = raw_area[:].rearrange("p n k i -> p (n k i)")[:, 0:NR * HB * D].rearrange("p (e k f) -> p e k f", e=NR, k=HB)
        xbcT = [sb(f"xbcT{i}", [P, NBLK, W]) for i in range(2)]
        zs = [sb(f"zs{i}", [P, DI]) for i in range(3)]
        xb = [sb(f"xb{i}", [P, DI + P]) for i in range(2)]
        gram = [sb(f"gram{i}", [P, P]) for i in range(2)]
        mix = [sb(f"mix{i}", [P, NH, P]) for i in range(2)]
        xdt = [sb(f"xdt{i}", [P, DI]) for i in range(2)]
        xend = [sb(f"xend{i}", [P, DI]) for i in range(2)]
        xskip = [sb(f"xskip{i}", [P, DI]) for i in range(2)]
        state = [sb(f"state{i}", [P, DI]) for i in range(2)]
        state_kept = sb("state_kept", [P, DI])
        y1 = [sb(f"y1_{i}", [P, DI]) for i in range(2)]
        y2 = [sb(f"y2_{i}", [P, DI]) for i in range(2)]
        g = [sb(f"g{i}", [P, DI]) for i in range(5)]
        squares = Ring([sb(f"squares{i}", [P, DI]) for i in range(2)])
        g_ss = sb("g_ss", [P, NC])
        g_rs = sb("g_rs", [P, NC])
        gT = [sb(f"gT{i}", [P, DI // P, P]) for i in range(2)]
        bn = sb("bn", [P, NC, 6])
        mv = sb("mv", [P, NC, 2])
        rstd = sb("rstd", [P, NC])
        x_ss = sb("x_ss", [P, NC])
        x_rs = sb("x_rs", [P, NC])
        x_rq = sb("x_rq", [P, NC])
        xn = [sb(f"xn{i}", [P, 4, D]) for i in range(2)]
        logits = sb("logits", [P, NC, NR])
        top_v = sb("top_v", [P, NC, 8])
        top_i = sb("top_i", [P, NC, 8], U32)
        top_f = sb("top_f", [P, NC, TOP_K])
        gates = sb("gates", [P, NC, NR])
        hot = sb("hot", [P, NC, NR])
        gsum = sb("gsum", [P, NC])
        gden = sb("gden", [P, NC])
        pick_v = sb("pick_v", [P, NC, TOP_K])
        hid = [sb(f"hid{i}", [P, HB, W]) for i in range(2)]
        banks = [ctx.enter_context(nc.psum_tensor(f"bank{i}", [P, BANK], F32)) for i in range(8)]

        act_banks, dve_banks = Ring(banks[:4]), Ring(banks[4:])

        def load(q, dst, src, signal):
            return q.put(lambda e: e.dma_start(dst, src), signal=signal, by=16)

        w1_v = w1_d.rearrange("p (e f) -> p e f", e=NE)
        w2_v = w2_d.rearrange("p (e k f) -> p e k f", e=NE, k=HB)
        xT_in = [None] * NB
        x_in = [None] * NB
        w_in_in = load(sp, w_in[:], w_in_d, "w_in_loaded")
        span = CPB * P
        xT_in[0] = load(sp, xT[:, 0:span], xT_d[:, 0:span], "xT0_loaded")
        params = [load(act, t[:], d, f"{n}_loaded") for n, t, d in (
            ("dt_bias", dt_bias, dt_bias_d), ("a_log", a_log, a_log_d), ("d_skip", d_skip, d_skip_d),
            ("conv_w", conv_w, conv_w_d), ("conv_b", conv_b, conv_b_d), ("norm_w", norm_w, norm_w_d),
            ("w_out", w_out, w_out_d), ("router", router, router_d), ("rms_w", rms_w, rms_w_d))]
        (dt_bias_in, a_log_in, d_skip_in, conv_w_in, conv_b_in, norm_w_in, w_out_in, router_in,
         rms_w_in) = params
        for b in range(NB):
            if b:
                xT_in[b] = load(sp, xT[:, b * span:(b + 1) * span], xT_d[:, b * span:(b + 1) * span],
                                f"xT{b}_loaded")
            x_in[b] = load(sp, x[:, b * CPB:(b + 1) * CPB, :], x_d[:, b * CPB:(b + 1) * CPB, :],
                           f"x{b}_loaded")
            if b == 1:
                w1_in = load(sp, w1_shared[:], w1_v[:, NR:], "w1_loaded")
                w2_in = load(sp, w2_shared[:], w2_v[:, NR:], "w2_loaded")

        def const(make, after=()):
            return pool.put(make, after=after, signal="consts")
        m1 = const(lambda e: e.memset(ones[:], 1.0))
        const(lambda e: e.memset(neg_half[:], -0.5))
        const(lambda e: e.memset(half[:], 0.5))
        const(lambda e: e.affine_select(out=upto[:], in_=ones[:], compare_op=ALU.is_ge, fill=0.0, base=0,
                                        pattern=[[1, P]], channel_multiplier=-1), [m1])
        const(lambda e: e.affine_select(out=beyond[:], in_=ones[:], compare_op=ALU.is_gt, fill=0.0, base=0,
                                        pattern=[[-1, P]], channel_multiplier=1))
        const(lambda e: e.affine_select(out=ident[:], in_=ones[:], compare_op=ALU.is_equal, fill=0.0, base=0,
                                        pattern=[[1, P]], channel_multiplier=-1))
        iota_done = const(lambda e: e.iota(expert_no_i[:], pattern=[[1, NR]], base=0, channel_multiplier=0))
        consts = const(lambda e: e.tensor_copy(expert_no[:], expert_no_i[:]), [iota_done])

        for k in range(DI // P):
            w_out_ready = dve.put(lambda e, k=k: e.tensor_scalar(w_out[:, k, :], w_out[:, k, :], norm_w[:, k:k + 1], None, ALU.mult),
                                  [w_out_in, norm_w_in], "w_out_scaled")
        neg_rate = act.put(lambda e: e.activation(a_rate[:], a_log[:], ACT.Exp), [a_log_in], "rate")
        rate = dve.put(lambda e: e.tensor_scalar(a_rate[:], a_rate[:], -1.0, None, ALU.mult), [neg_rate], "rate_negated")

        def wide(ap, n):
            return ap.unsqueeze(len(ap.shape)).to_broadcast(list(ap.shape) + [n])

        def steps_of(c0, c1):
            n = c1 - c0
            _, bank, free = dve_banks.take()
            raw_dt = bank[:, 0:n * NH].rearrange("p (c h) -> p c h", h=NH)
            for c in range(c0, c1):
                made = pe.put(lambda e, c=c: e.matmul(raw_dt[:, c - c0, :], xT[:, c * P:(c + 1) * P],
                                                      w_in[:, w_in.shape[1] - NH:], start=True, stop=True),
                              [w_in_in, xT_in[c // CPB], *free], "dt_raw")
            cut = slice(c0, c1)
            v, s, p, q, t = (a[:, cut, :] for a in (dt_raw, dt_s, dt_p, dt_q, dt))
            bias = dt_bias[:].unsqueeze(1).to_broadcast([P, n, NH])
            d = dve.put(lambda e: e.tensor_tensor(v, raw_dt, bias, ALU.add), [made, dt_bias_in], "dt")
            dve_banks.free[dve_banks.at] = (d,)
            d = dve.put(lambda e: e.scalar_tensor_tensor(q, v, -1.0, v, ALU.mult, ALU.min), [d], "dt")
            a = act.put(lambda e: e.activation(s, q, ACT.Exp), [d], "dt_exp")
            d = dve.put(lambda e: e.tensor_scalar(q, s, 2.0, None, ALU.add), [a], "dt")
            d = dve.put(lambda e: e.reciprocal(q, q), [d], "dt")
            d = dve.put(lambda e: e.tensor_tensor(s, s, q, ALU.mult), [d], "dt")
            d = dve.put(lambda e: e.tensor_tensor(q, s, s, ALU.mult), [d], "dt")
            d = dve.put(lambda e: e.tensor_scalar(p, q, 1.0 / (2 * LOG1P_TERMS + 1), None, ALU.mult), [d], "dt")
            for k in range(LOG1P_TERMS - 1, 0, -1):
                d = dve.put(lambda e, k=k: e.scalar_tensor_tensor(p, p, 1.0 / (2 * k + 1), q, ALU.add, ALU.mult), [d], "dt")
            d = dve.put(lambda e: e.scalar_tensor_tensor(p, p, 1.0, s, ALU.add, ALU.mult), [d], "dt")
            d = dve.put(lambda e: e.tensor_scalar(v, v, 0.0, None, ALU.max), [d], "dt")
            d = dve.put(lambda e: e.scalar_tensor_tensor(t, p, 2.0, v, ALU.mult, ALU.add), [d], "dt")
            al = a_log_step[:, cut, :]
            rates = a_rate[:].unsqueeze(1).to_broadcast([P, n, NH])
            d = dve.put(lambda e: e.tensor_tensor(al, t, rates, ALU.mult), [d, rate], "dt")
            d = dve.put(lambda e: e.tensor_scalar(al, al, A_FLOOR, None, ALU.max), [d], "dt")
            for lhs, dst in ((upto, into), (beyond, outof), (ones, whole)):
                i, bank, free = act_banks.take()
                s_ps = bank[:, 0:n * NH]
                m = pe.put(lambda e, lhs=lhs, s_ps=s_ps: e.matmul(s_ps, lhs[:], a_log_step[:, cut, :].rearrange("p c h -> p (c h)"), start=True, stop=True),
                           [d, consts, *free], "chunk_sums")
                a = act.put(lambda e, dst=dst, s_ps=s_ps: e.activation(dst[:, cut, :].rearrange("p c h -> p (c h)"), s_ps, ACT.Exp), [m], "chunk_decays")
                act_banks.free[i] = (a,)
            return d, a

        arow_free = [None, None]
        decay_free = [None] * len(decay)

        def decays_of(c, steps):
            buf, slot = arow[c % 2], c % len(decay)
            one = pool.put(lambda e: e.tensor_tensor(buf[:], upto[:].unsqueeze(1).to_broadcast([P, NH, P]),
                                                     a_log_step[:, c, :].unsqueeze(2).to_broadcast([P, NH, P]), ALU.mult),
                           [steps[0], consts, arow_free[c % 2]], "arow")
            i, bank, free = act_banks.take()
            m = pe.put(lambda e: e.matmul(bank[:], beyond[:], buf[:].rearrange("p h i -> p (h i)"), start=True, stop=True),
                       [one, *free], "segment_sums")
            arow_free[c % 2] = m
            a = act.put(lambda e: e.activation(decay[slot].rearrange("p h i -> p (h i)"), bank[:], ACT.Exp),
                        [m, decay_free[slot]], "decays")
            act_banks.free[i] = (a,)
            return a

        raw_free = [[], []]
        xbc_free = [[], []]
        raw_done = [None] * NT

        def conv_of(t):
            b, r, o = t // TPB, raw[t % 2], xbcT[t % 2]
            if t % TPB == 0:
                halo = pool.put(lambda e: e.memset(r[:, :, 0:TAPS - 1], 0.0), raw_free[t % 2], "halo")
            else:
                prev = raw[(t - 1) % 2]
                halo = pool.put(lambda e: e.tensor_copy(r[:, :, 0:TAPS - 1], prev[:, :, W:W + TAPS - 1]),
                                [*raw_free[t % 2], raw_done[t - 1]], "halo")
            freed, done = [halo] if t % TPB else [], []
            for k in range(NBLK):
                i, bank, free = act_banks.take()
                m = pe.put(lambda e, k=k, bank=bank: e.matmul(bank[:], w_in[:, DI + k * P:DI + (k + 1) * P], xT[:, t * W:(t + 1) * W], start=True, stop=True),
                           [xT_in[b], w_in_in, *free], "xbc")
                a = act.put(lambda e, k=k, bank=bank: e.activation(r[:, k, TAPS - 1:], bank[:], ACT.Copy), [m, *raw_free[t % 2]], "xbc_raw")
                act_banks.free[i] = (a,)
                raw_done[t] = a
                d = dve.put(lambda e, k=k: e.tensor_scalar(o[:, k, :], r[:, k, 0:W], conv_w[:, k, TAPS - 1:TAPS], conv_b[:, k:k + 1], ALU.mult, ALU.add),
                            [a, halo, conv_w_in, conv_b_in, *xbc_free[t % 2]], "conv")
                for n in range(1, TAPS):
                    d = dve.put(lambda e, k=k, n=n: e.scalar_tensor_tensor(o[:, k, :], r[:, k, n:n + W], conv_w[:, k, TAPS - 1 - n:TAPS - n], o[:, k, :], ALU.mult, ALU.add), [d], "conv")
                freed.append(d)
                done.append(act.put(lambda e, k=k: e.activation(o[:, k, :], o[:, k, :], ACT.Silu), [d], "xbc_silu"))
            raw_free[(t - 1) % 2] = raw_free[(t - 1) % 2] + [halo]
            raw_free[t % 2] = [d]
            return done[-1]

        zs_free = [None] * 3

        def z_of(c):
            i, bank, free = act_banks.take()
            m = pe.put(lambda e: e.matmul(bank[:, 0:DI], xT[:, c * P:(c + 1) * P], w_in[:, 0:DI], start=True, stop=True),
                       [xT_in[c // CPB], w_in_in, *free], "z")
            a = act.put(lambda e: e.activation(zs[c % 3][:], bank[:, 0:DI], ACT.Silu), [m, zs_free[c % 3]], "z_silu")
            act_banks.free[i] = (a,)
            return a, m

        free_xb, free_gram, free_mix, free_xdt, free_xend, free_xskip, free_y = ([()] * 2 for _ in range(7))
        state_done = [None] * NC
        state_read = [()] * NC
        g_free = [()] * 5

        def sum_squares(dst, src, after):
            i, buf, free = squares.take()
            a = act.put(lambda e: e.activation(buf[:, 0:src.shape[1]], src, ACT.Square, accum_out=dst), [after, *free], "squares")
            squares.free[i] = (a,)
            return a

        def scan_a(c, xbc, dec):
            o, at, h = xbcT[c // 4 % 2], (c % 4) * P, c % 2
            i, bank, free = dve_banks.take()
            for k in range(3):
                m = pe.put(lambda e, k=k: e.transpose(bank[:, k * P:(k + 1) * P], o[:, k, at:at + P], ident[:]), [xbc, consts, *free], "token_major")
            m = pe.put(lambda e: e.matmul(bank[:, 3 * P:4 * P], o[:, 2, at:at + P], o[:, 3, at:at + P], start=True, stop=True), [], "token_major")
            d1 = dve.put(lambda e: e.tensor_copy(xb[h][:], bank[:, 0:3 * P]), [m, *free_xb[h]], "xb")
            d2 = dve.put(lambda e: e.tensor_tensor(gram[h][:], bank[:, 3 * P:4 * P], upto[:], ALU.mult), [m, *free_gram[h], consts], "gram")
            dve_banks.free[i] = (d1, d2)
            slot = c % len(decay)
            d3 = dve.put(lambda e: e.tensor_tensor(mix[h][:], decay[slot], gram[h][:].unsqueeze(1).to_broadcast([P, NH, P]), ALU.mult),
                         [dec, d2, *free_mix[h]], "mix")
            decay_free[slot] = d3
            free_gram[h] = (d3,)
            xv = xb[h][:, 0:DI].rearrange("p (h e) -> p h e", h=NH)

            def per_head(dst, a, s, after, signal):
                return pool.put(lambda e: e.tensor_tensor(dst[:].rearrange("p (h e) -> p h e", h=NH), a, s.unsqueeze(2).to_broadcast([P, NH, HD]), ALU.mult), after, signal)
            p1 = per_head(xdt[h], xv, dt[:, c, :], [d1, *free_xdt[h]], "xdt")
            p2 = per_head(xend[h], xdt[h][:].rearrange("p (h e) -> p h e", h=NH), outof[:, c, :], [p1, *free_xend[h]], "xend")
            p3 = per_head(xskip[h], xv, d_skip[:], [d_skip_in, *free_xskip[h]], "xskip")
            free_xb[h] = (p1, p3)
            return d3, p1, p2, p3, d1, m

        def scan_b(c, made, z):
            d3, p1, p2, p3, d1, tm = made
            o, at, h = xbcT[c // 4 % 2], (c % 4) * P, c % 2
            first = c % CPB == 0
            iu, ubank, ufree = dve_banks.take()
            mu = pe.put(lambda e: e.matmul(ubank[:, 0:DI], xb[h][:, DI:DI + P], xend[h][:], start=True, stop=True), [p2, d1, *ufree], "state_add")
            free_xend[h] = (mu,)
            free_xb[h] = (*free_xb[h], mu)
            iy, ybank, yfree = dve_banks.take()
            for k in range(NH):
                my = pe.put(lambda e, k=k: e.matmul(ybank[:, k * HD:(k + 1) * HD], mix[h][:, k, :], xdt[h][:, k * HD:(k + 1) * HD], start=True, stop=True),
                            [d3, p1, *yfree], "y_inside")
            if not first:
                my = pe.put(lambda e: e.matmul(ybank[:, DI:2 * DI], o[:, 3, at:at + P], state[(c - 1) % 2][:], start=True, stop=True), [state_done[c - 1]], "y_carried")
                state_read[c - 1] = (my,)
            free_mix[h] = (my,)
            free_xdt[h] = (my, p2)
            before = list(state_read[c - 2]) if c >= 2 else []
            if first:
                ds = dve.put(lambda e: e.tensor_copy(state[c % 2][:], ubank[:, 0:DI]), [mu, *before], "state")
            else:
                wh = whole[:, c, :].unsqueeze(2).to_broadcast([P, NH, HD])
                v = lambda a: a[:].rearrange("p (h e) -> p h e", h=NH)
                pk = pool.put(lambda e: e.tensor_tensor(v(state_kept), v(state[(c - 1) % 2]), wh, ALU.mult), [state_done[c - 1]], "state_kept")
                ds = dve.put(lambda e: e.tensor_tensor(state[c % 2][:], ubank[:, 0:DI], state_kept[:], ALU.add), [mu, pk, *before], "state")
                state_read[c - 1] = (*state_read[c - 1], pk)
            state_done[c] = ds
            dve_banks.free[iu] = (ds,)
            if first:
                dy = dve.put(lambda e: e.tensor_tensor(y2[h][:], ybank[:, 0:DI], xskip[h][:], ALU.add), [my, p3, *free_y[h]], "y")
                y = y2[h]
            else:
                carried = ybank[:, DI:2 * DI].rearrange("p (h e) -> p h e", h=NH)
                e_in = into[:, c, :].unsqueeze(2).to_broadcast([P, NH, HD])
                da = dve.put(lambda e: e.tensor_tensor(y1[h][:].rearrange("p (h e) -> p h e", h=NH), carried, e_in, ALU.mult), [my, *free_y[h]], "y")
                dy = dve.put(lambda e: e.tensor_tensor(y2[h][:], ybank[:, 0:DI], xskip[h][:], ALU.add), [p3], "y")
                y = y1[h]
            dve_banks.free[iy] = (dy,)
            free_xskip[h] = (dy,)
            if not first:
                dy = dve.put(lambda e: e.tensor_tensor(y1[h][:], y1[h][:], y2[h][:], ALU.add), [dy], "y")
            gi = c % 5
            dg = dve.put(lambda e: e.tensor_tensor(g[gi][:], y[:], zs[c % 3][:], ALU.mult), [dy, z, *g_free[gi]], "gated")
            zs_free[c % 3] = dg
            free_y[h] = (dg,)
            a = sum_squares(g_ss[:, c:c + 1], g[gi][:], dg)
            if c % 4 == 3:
                xbc_free[c // 4 % 2] = [my, tm]
            return dg, a

        gT_free = [None, None]

        def pow_of(dst, src, mul, add, power, after, signal):
            n = src.shape[1]
            one = pool.put(lambda e: e.tensor_scalar(dst, src, mul, add, ALU.mult, ALU.add), after, signal)
            return pool.put(lambda e: e.tensor_tensor(dst, dst, power[:, 0:n], ALU.pow), [one], signal)

        def project(t, gated):
            c0 = 4 * t
            rs = pow_of(g_rs[:, c0:c0 + 4], g_ss[:, c0:c0 + 4], 1.0 / DI, LN_EPS, neg_half, [gated[-1][1]], "g_rs")
            for c in range(c0, c0 + 4):
                gi = c % 5
                i, bank, free = act_banks.take()
                for k in range(DI // P):
                    m = pe.put(lambda e, k=k, bank=bank, gi=gi: e.transpose(bank[:, k * P:(k + 1) * P], g[gi][:, k * P:(k + 1) * P], ident[:]), [gated[c - c0][0], *free], "gT")
                g_free[gi] = (m, gated[c - c0][1])
                a = act.put(lambda e, bank=bank, c=c: e.activation(gT[c % 2][:].rearrange("p k i -> p (k i)"), bank[:, 0:DI], ACT.Copy), [m, gT_free[c % 2]], "gT_copied")
                act_banks.free[i] = (a,)
                i, bank, free = dve_banks.take()
                for k in range(DI // P):
                    m = pe.put(lambda e, k=k, bank=bank, c=c: e.matmul(bank[:, 0:D], gT[c % 2][:, k, :], w_out[:, k, :], start=(k == 0), stop=(k == DI // P - 1)), [a, w_out_ready, *free], "out_proj")
                gT_free[c % 2] = m
                d = dve.put(lambda e, bank=bank, c=c: e.scalar_tensor_tensor(x[:, c, :], bank[:, 0:D], g_rs[:, c:c + 1], x[:, c, :], ALU.mult, ALU.add), [m, rs, x_in[c // CPB]], "residual")
                dve_banks.free[i] = (d,)
                d = dve.put(lambda e, c=c: e.bn_stats(bn[:, c, :], x[:, c, :]), [d], "ln_stats")
                d = dve.put(lambda e, c=c: e.bn_aggr(mv[:, c, :], bn[:, c, :]), [d], "ln_stats")
            return d

        def normalise(t, stats, signal):
            c0 = 4 * t
            r = pow_of(rstd[:, c0:c0 + 4], mv[:, c0:c0 + 4, 1], 1.0, LN_EPS, neg_half, [stats], signal + "_rstd")
            for c in range(c0, c0 + 4):
                d = dve.put(lambda e, c=c: e.tensor_scalar(x[:, c, :], x[:, c, :], mv[:, c, 0:1], rstd[:, c:c + 1], ALU.subtract, ALU.mult), [r, stats], signal)
            return d

        xn_free = [None, None]
        expert_in = [None] * NT
        logits_done = [None] * NT

        def prepare(t, stats, z_read):
            c0 = 4 * t
            d = normalise(t, stats, "x1")
            for c in range(c0, c0 + 4):
                a = sum_squares(x_ss[:, c:c + 1], x[:, c, :], d)
            cut = slice(c0, c0 + 4)
            rs = pow_of(x_rs[:, cut], x_ss[:, cut], 1.0 / D, RMS_EPS, neg_half, [a], "x_rs")
            rq = pow_of(x_rq[:, cut], x_ss[:, cut], 1.0 / D, RMS_EPS, half, [a], "x_rs")
            for c in range(c0, c0 + 4):
                d = dve.put(lambda e, c=c: e.tensor_scalar(xn[t % 2][:, c - c0, :], x[:, c, :], x_rs[:, c:c + 1], None, ALU.mult), [rs, xn_free[t % 2]], "xn")
            i, bank, free = dve_banks.take()
            for k in range(4):
                m = pe.put(lambda e, k=k: e.transpose(bank[:, k * P:(k + 1) * P], xn[t % 2][:, k, :], ident[:]), [d, *free], "xnT")
            xn_free[t % 2] = m
            d = dve.put(lambda e: e.tensor_copy(xT[:, t * W:(t + 1) * W], bank[:]), [m, z_read], "xnT_copied")
            dve_banks.free[i] = (d,)
            expert_in[t] = d
            i, bank, free = dve_banks.take()
            for k in range(4):
                m = pe.put(lambda e, k=k, bank=bank: e.matmul(bank[:, k * NR:(k + 1) * NR], xT[:, (c0 + k) * P:(c0 + k + 1) * P], router[:], start=True, stop=True), [d, router_in, *free], "router")
            dl = dve.put(lambda e, bank=bank: e.tensor_tensor(logits[:, cut, :], bank[:, 0:4 * NR].rearrange("p (c r) -> p c r", c=4), x_rq[:, cut].unsqueeze(2).to_broadcast([P, 4, NR]), ALU.mult), [m, rq], "logits")
            dve_banks.free[i] = (dl,)
            for c in range(c0, c0 + 4):
                d1 = dve.put(lambda e, c=c: e.max(top_v[:, c, :], logits[:, c, :]), [dl], "top")
                d1 = dve.put(lambda e, c=c: e.max_index(top_i[:, c, :], top_v[:, c, :], logits[:, c, :]), [d1], "top")
            logits_done[t] = d1

        hid_free = [None, None]
        hid_n = [0]
        acc_done = [None] * NT

        def hidden(e_no, t):
            hb = hid_n[0] % 2
            hid_n[0] += 1
            for k in range(HB):
                i, bank, free = act_banks.take()
                m = pe.put(lambda e, k=k, bank=bank: e.matmul(bank[:], w1_of(e_no)[:, k * P:(k + 1) * P], xT[:, t * W:(t + 1) * W], start=True, stop=True),
                           [w1_scaled[e_no >= NR], expert_in[t], *free], "hidden")
                a = act.put(lambda e, k=k, bank=bank: e.activation(hid[hb][:, k, :], bank[:], ACT.Silu), [m, hid_free[hb]], "hidden_silu")
                act_banks.free[i] = (a,)
            return hb, a

        def down(e_no, bank, c, hb, after, start, stop):
            for k in range(HB):
                m = pe.put(lambda e, k=k: e.matmul(bank[:, c * P:(c + 1) * P], hid[hb][:, k, c * P:(c + 1) * P], w2_of(e_no)[:, k, :], start=(start and k == 0), stop=(stop and k == HB - 1)),
                           [w2_loaded[e_no >= NR], *after], "down")
            return m

        w1_scaled = [None, None]
        w2_loaded = [None, w2_in]

        def w1_of(n):
            return w1_routed[:, n] if n < NR else w1_shared[:, n - NR]

        def w2_of(n):
            return w2_routed[:, n] if n < NR else w2_shared[:, n - NR]

        def scale_w1(nos, loaded):
            for k in nos:
                made = dve.put(lambda e, k=k: e.tensor_scalar(w1_of(k), w1_of(k), rms_w[:, k:k + 1], None, ALU.mult), [loaded, rms_w_in], "w1_scaled")
            return made

        def shared(t):
            made = [hidden(e_no, t) for e_no in range(NR, NE)]
            i, bank, free = dve_banks.take()
            for c in range(4):
                for n, (hb, a) in enumerate(made):
                    m = down(NR + n, bank, c, hb, [a, *free], n == 0, n == NE - NR - 1)
            for hb, _ in made:
                hid_free[hb] = m
            acc_done[t] = dve.put(lambda e: e.tensor_tensor(x[:, 4 * t:4 * t + 4, :], bank[:].rearrange("p (c d) -> p c d", c=4), x[:, 4 * t:4 * t + 4, :], ALU.add), [m], "shared_added")
            dve_banks.free[i] = (acc_done[t],)

        def gate_weights():
            v2 = top_v[:, :, 0:TOP_K]
            d = dve.put(lambda e: e.tensor_copy(top_f[:], top_i[:, :, 0:TOP_K]), [logits_done[-1]], "gate")
            d = dve.put(lambda e: e.tensor_tensor(gates[:], logits[:], top_v[:, :, 0:1].to_broadcast([P, NC, NR]), ALU.subtract), [], "gate")
            d = dve.put(lambda e: e.tensor_tensor(pick_v[:], v2, top_v[:, :, 0:1].to_broadcast([P, NC, TOP_K]), ALU.subtract), [], "gate")
            a = act.put(lambda e: e.activation(gates[:], gates[:], ACT.Exp), [d], "gate_exp")
            a = act.put(lambda e: e.activation(pick_v[:], pick_v[:], ACT.Exp), [], "gate_exp")
            d = dve.put(lambda e: e.tensor_reduce(gsum[:], gates[:], AX.X, ALU.add), [a], "gate")
            d = dve.put(lambda e: e.reciprocal(gsum[:], gsum[:]), [d], "gate")
            d = dve.put(lambda e: e.tensor_tensor(pick_v[:], pick_v[:], gsum[:].unsqueeze(2).to_broadcast([P, NC, TOP_K]), ALU.mult), [d], "gate")
            d = dve.put(lambda e: e.tensor_reduce(gden[:], pick_v[:], AX.X, ALU.add), [d], "gate")
            d = dve.put(lambda e: e.tensor_scalar(gden[:], gden[:], GATE_EPS, None, ALU.add), [d], "gate")
            d = dve.put(lambda e: e.reciprocal(gden[:], gden[:]), [d], "gate")
            d = dve.put(lambda e: e.tensor_tensor(pick_v[:], pick_v[:], gden[:].unsqueeze(2).to_broadcast([P, NC, TOP_K]), ALU.mult), [d], "gate")
            for k in range(TOP_K):
                dst = gates if k == 0 else hot
                nos = expert_no[:].unsqueeze(1).to_broadcast([P, NC, NR])
                d = dve.put(lambda e, k=k, dst=dst: e.tensor_tensor(dst[:], nos, top_f[:, :, k:k + 1].to_broadcast([P, NC, NR]), ALU.is_equal), [d, consts], "gate")
                d = dve.put(lambda e, k=k, dst=dst: e.tensor_tensor(dst[:], dst[:], pick_v[:, :, k:k + 1].to_broadcast([P, NC, NR]), ALU.mult), [d], "gate")
            return dve.put(lambda e: e.tensor_tensor(gates[:], gates[:], hot[:], ALU.add), [d], "gate")

        def routed(t, gate):
            for e_no in range(NR):
                hb, a = hidden(e_no, t)
                i, bank, free = dve_banks.take()
                for c in range(4):
                    m = down(e_no, bank, c, hb, [a, *free], True, True)
                hid_free[hb] = m
                for c in range(4 * t, 4 * t + 4):
                    d = dve.put(lambda e, c=c, bank=bank, e_no=e_no: e.scalar_tensor_tensor(x[:, c, :], bank[:, (c % 4) * P:(c % 4 + 1) * P], gates[:, c, e_no:e_no + 1], x[:, c, :], ALU.mult, ALU.add),
                                [m, gate, acc_done[t]], "routed_added")
                dve_banks.free[i] = (d,)
                acc_done[t] = d

        def finish(t):
            for c in range(4 * t, 4 * t + 4):
                d = dve.put(lambda e, c=c: e.bn_stats(bn[:, c, :], x[:, c, :]), [acc_done[t]], "ln_stats")
                d = dve.put(lambda e, c=c: e.bn_aggr(mv[:, c, :], bn[:, c, :]), [d], "ln_stats")
            d = normalise(t, d, "x2")
            return sp.put(lambda e: e.dma_start(out_d[:, 4 * t:4 * t + 4, :], x[:, 4 * t:4 * t + 4, :]), [d], "stored", 16)

        head = steps_of(0, CPB)
        dec = {c: decays_of(c, head) for c in range(CPB)}
        rest = steps_of(CPB, NC)
        w1_scaled[1] = scale_w1(range(NR, NE), w1_in)
        xbc = {0: conv_of(0)}
        zt, sa, gated, z_read, stats = {}, {}, {}, {}, {}
        for c in range(NC + 12):
            t, k = c // 4, c % 4
            if c < NC:
                zt[c] = z_of(c)
                sa[c] = scan_a(c, xbc[t], dec[c])
            if 1 <= c <= NC:
                gated[c - 1] = scan_b(c - 1, sa[c - 1], zt[c - 1][0])
            if k == 1 and t + 1 < NT:
                xbc[t + 1] = conv_of(t + 1)
            if k == 1 and 1 <= t <= NT:
                stats[t - 1] = project(t - 1, [gated[4 * (t - 1) + j] for j in range(4)])
            if k == 3 and 1 <= t <= NT:
                prepare(t - 1, stats[t - 1], zt[4 * t - 1][1])
            if k == 1 and 2 <= t <= NT + 1:
                shared(t - 2)
            if c % CPB == CPB - 2 and c + 2 < NC:
                b = c // CPB + 1
                for n in range(b * CPB, (b + 1) * CPB):
                    dec[n] = decays_of(n, rest)
        w2_loaded[0] = sp.put(lambda e: e.dma_start(w2_routed, w2_v[:, 0:NR]), [*raw_free[0], *raw_free[1]], "w2r_loaded", 16)
        w1r_in = sp.put(lambda e: e.dma_start(w1_routed, w1_v[:, 0:NR]), decay_free, "w1r_loaded", 16)
        gate = gate_weights()
        w1_scaled[0] = scale_w1(range(NR), w1r_in)
        for t in range(NT):
            routed(t, gate)
            last = finish(t)
        sp.put(lambda e: e.nop(), [last])

        semaphores = {n: ctx.enter_context(nc.semaphore(n)) for n in counts}
        block = ctx.enter_context(nc.Block())

        @block.sync
        def _(e):
            sp.play(e, semaphores)

        @block.scalar
        def _(e):
            act.play(e, semaphores)

        @block.vector
        def _(e):
            dve.play(e, semaphores)

        @block.gpsimd
        def _(e):
            pool.play(e, semaphores)

        @block.tensor
        def _(e):
            pe.play(e, semaphores)


def kernel(**inputs):
    import numpy as np
    import concourse.bacc as bacc
    from concourse.bass_utils import run_bass_kernel_spmd

    a = {n: np.asarray(v) for n, v in inputs.items()}
    x = a["L0_attn_x"]
    nb, length, d = x.shape
    tokens = x.reshape(nb * length, d)
    chunks = tokens.shape[0] // P

    def channels(v, n=P):
        return np.moveaxis(v.reshape(*v.shape[:-1], -1, n), -1, 0)

    def rows(v):
        return np.broadcast_to(v[None], (P, *v.shape))

    w1 = np.concatenate([a["L0_ffn_w1"], a["L0_ffn_w1_s"]])
    w2 = np.concatenate([a["L0_ffn_w2"], a["L0_ffn_w2_s"]])
    rms = np.concatenate([a["L0_ffn_rms_w"], a["L0_ffn_rms_w_s"]])
    arrays = {
        "xT": tokens.T,
        "x": tokens.reshape(chunks, P, d).transpose(1, 0, 2),
        "w_in": a["L0_attn_in_proj_w"],
        "conv_w": channels(a["L0_attn_conv_w"]).transpose(0, 2, 1),
        "conv_b": channels(a["L0_attn_conv_b"]),
        "norm_w": channels(a["L0_attn_norm_w"]),
        "w_out": a["L0_attn_out_proj_w"].reshape(-1, P, d).transpose(1, 0, 2),
        "dt_bias": rows(a["L0_attn_dt_bias"]),
        "a_log": rows(a["L0_attn_A_log"]),
        "d_skip": rows(a["L0_attn_D"]),
        "router": a["L0_ffn_router_w"],
        "rms_w": rms.T,
        "w1": w1.transpose(1, 0, 2).reshape(d, -1),
        "w2": w2.reshape(w2.shape[0], -1, P, d).transpose(2, 0, 1, 3).reshape(P, -1),
    }
    arrays = {n: np.ascontiguousarray(v) for n, v in arrays.items()}
    nc = bacc.Bacc("TRN2", target_bir_lowering=False, num_devices=1)
    args = [nc.dram_tensor(n + "_dram", v.shape, F32, kind="ExternalInput").ap() for n, v in arrays.items()]
    out = nc.dram_tensor("out_dram", (P, chunks, d), F32, kind="ExternalOutput").ap()
    mamba_moe(nc, *args, out)
    r = run_bass_kernel_spmd(nc, [{n + "_dram": v for n, v in arrays.items()}], core_ids=[0])
    got = r.results[0]["out_dram"]
    return np.ascontiguousarray(got.transpose(1, 0, 2)).reshape(nb, length, d)
```

```python
from contextlib import ExitStack

import concourse.bass as bass
from concourse import mybir

F32 = mybir.dt.float32
F32R = mybir.dt.float32r
BF16 = mybir.dt.bfloat16
I32 = mybir.dt.int32
U32 = mybir.dt.uint32
ET = mybir.EngineType
ALU = mybir.AluOpType
ACT = mybir.ActivationFunctionType
AX = mybir.AxisListType
P = 128
BANK = 512
TAPS = 4
TOP_K = 2
LN_EPS = 1e-5
RMS_EPS = 1.1920929e-07
GATE_EPS = 1e-9
A_FLOOR = -200.0
LOG1P_TERMS = 8


class Queue:

    def __init__(self, name, counts):
        self.name, self.steps, self.seen, self.counts = name, [], {}, counts

    def put(self, make, after=(), signal=None, by=1):
        waits = []
        for done in after:
            if done is not None and self.seen.get(done[0], 0) < done[1]:
                self.seen[done[0]] = done[1]
                waits.append(done)
        token = None
        if signal is not None:
            self.counts[signal] = self.counts.get(signal, 0) + by
            token = (signal, self.counts[signal])
        self.steps.append((waits, make, signal, by))
        return token

    def play(self, engine, semaphores):
        for waits, make, signal, by in self.steps:
            for name, value in waits:
                engine.wait_ge(semaphores[name], value)
            made = make(engine)
            if signal is not None:
                made.then_inc(semaphores[signal], by)


class Ring:

    def __init__(self, buffers):
        self.buffers, self.free, self.at = buffers, [()] * len(buffers), -1

    def take(self):
        self.at = (self.at + 1) % len(self.buffers)
        return self.at, self.buffers[self.at], self.free[self.at]


def mamba_moe(nc, xT_d, x_d, w_in_d, conv_w_d, conv_b_d, norm_w_d, w_out_d, dt_bias_d, a_log_d,
              d_skip_d, router_d, rms_w_d, w1_d, w2_d, out_d):
    D = xT_d.shape[0]
    TOK = xT_d.shape[1]
    NB = 8
    NC = TOK // P
    CPB = NC // NB
    NT = NC // 4
    TPB = NT // NB
    NH = dt_bias_d.shape[1]
    DI = norm_w_d.shape[1] * P
    HD = DI // NH
    NBLK = conv_b_d.shape[1]
    NE = w1_d.shape[1] // (2 * P)
    NR = router_d.shape[1]
    HB = 2
    W = 4 * P
    REGION = TOK + P
    SLOT_TILES = -(-(TOP_K * TOK // P + NR - 1) // 8) * 8
    NOWHERE = TOP_K * TOK
    dispatched = nc.dram_tensor("dispatched", [(NR + 1) * REGION, D + 1], F32, kind="Internal").ap()
    returned = nc.dram_tensor("returned", [TOP_K * TOK, D], F32, kind="Internal").ap()

    counts = {}
    pe, act, dve, pool, sp = (Queue(n, counts) for n in ("pe", "act", "dve", "pool", "sp"))

    with ExitStack() as ctx:
        def sb(name, shape, dt=F32):
            return ctx.enter_context(nc.sbuf_tensor(name, shape, dt))

        xT = sb("xT", [P, TOK])
        x = sb("x", [P, NC, D])
        w_in = sb("w_in", [P, w_in_d.shape[1]])
        conv_w = sb("conv_w", [P, NBLK, TAPS])
        conv_b = sb("conv_b", [P, NBLK])
        norm_w = sb("norm_w", [P, DI // P])
        w_out = sb("w_out", [P, DI // P, D])
        dt_bias = sb("dt_bias", [P, NH])
        a_log = sb("a_log", [P, NH])
        d_skip = sb("d_skip", [P, NH])
        router = sb("router", [P, P])
        rms_w = sb("rms_w", [P, NE])
        w1_shared = sb("w1_shared", [P, NE - NR, HB * P])
        w2_shared = sb("w2_shared", [P, NE - NR, HB, D])
        ident = sb("ident", [P, P])
        upto = sb("upto", [P, P])
        beyond = sb("beyond", [P, P])
        beyond_r = sb("beyond_r", [P, P], F32R)
        before_b = sb("before_b", [P, P], BF16)
        ones = sb("ones", [P, P])
        ones_b = sb("ones_b", [P, P], BF16)
        neg_half = sb("neg_half", [P, 8])
        expert_no = sb("expert_no", [P, NR])
        expert_no_i = sb("expert_no_i", [P, NR], I32)
        first_row = sb("first_row", [P, NR])
        a_rate = sb("a_rate", [P, NH])
        dt = sb("dt", [P, NC, NH])
        a_log_step = sb("a_log_step", [P, NC, NH])
        a_hi = sb("a_hi", [P, NC, NH], F32R)
        a_lo = sb("a_lo", [P, NC, NH], F32R)
        into = sb("into", [P, NC, NH])
        outof = sb("outof", [P, NC, NH])
        whole = sb("whole", [P, NC, NH])
        arow = [[sb(f"arow{i}_{n}", [P, NH, P], F32R) for n in ("hi", "lo")] for i in range(2)]
        decay_area = sb("decay_area", [P, CPB + 3, NH, P])
        decay = [decay_area[:, i] for i in range(CPB + 3)]
        w1_routed = decay_area[:].rearrange("p n h i -> p (n h i)")[:, 0:NR * HB * P].rearrange("p (e f) -> p e f", e=NR)
        gexp = decay_area[:].rearrange("p n h i -> p (n h i)")[:, NR * HB * P:NR * HB * P + NC * NR].rearrange("p (c r) -> p c r", c=NC)
        raw = [sb(f"raw{i}", [P, TAPS - 1 + W]) for i in range(3)]
        tail = sb("tail", [P, NBLK, TAPS - 1])
        xbcT_area = sb("xbcT_area", [P, 2, NBLK, W])
        xbcT = [xbcT_area[:, i] for i in range(2)]
        w2_routed = xbcT_area[:].rearrange("p n k i -> p (n k i)")[:, 0:NR * HB * D].rearrange("p (e f) -> p e f", e=NR)
        zs = [sb(f"zs{i}", [P, DI]) for i in range(4)]
        xb = [sb(f"xb{i}", [P, DI + P]) for i in range(2)]
        gram = [sb(f"gram{i}", [P, P]) for i in range(2)]
        mix = [sb(f"mix{i}", [P, NH, P]) for i in range(2)]
        xdt = [sb(f"xdt{i}", [P, DI + HD]) for i in range(2)]
        xend = [sb(f"xend{i}", [P, DI]) for i in range(2)]
        xskip = sb("xskip", [P, DI])
        state = [sb(f"state{i}", [P, DI]) for i in range(2)]
        state_kept = sb("state_kept", [P, DI])
        y_carried = sb("y_carried", [P, DI])
        y_inside = sb("y_inside", [P, DI])
        g = [sb(f"g{i}", [P, DI]) for i in range(3)]
        squares = Ring([sb(f"squares{i}", [P, DI], BF16) for i in range(2)])
        g_ss = sb("g_ss", [P, NC])
        g_rs = sb("g_rs", [P, NC])
        gT = [sb(f"gT{i}", [P, DI // P, P]) for i in range(2)]
        bn = sb("bn", [P, NC, 6])
        mv = sb("mv", [P, NC, 2])
        rstd = sb("rstd", [P, NC])
        x_ss = sb("x_ss", [P, NC])
        x_ms = sb("x_ms", [P, NC])
        x_rs = sb("x_rs", [P, NC])
        x_rq = sb("x_rq", [P, NC])
        ROW = D + 1
        rows = [sb(f"rows{i}", [P, TOP_K, 4, ROW]) for i in range(2)]
        filler = sb("filler", [P, ROW])
        xnT = [sb(f"xnT{i}", [P, W]) for i in range(3)]
        logits = sb("logits", [P, NC, NR])
        top_v = sb("top_v", [P, NC, 8])
        top_i = sb("top_i", [P, 4, 8], U32)
        top_f = sb("top_f", [P, 4, TOP_K])
        hot = sb("hot", [P, TOP_K, 4, NR])
        chosen = [sb(f"chosen{i}", [P, 5, NR], BF16) for i in range(2)]
        next_row = [sb(f"next_row{i}", [P, NR]) for i in range(2)]
        row_of = sb("row_of", [P, 4, NR])
        row_hot = sb("row_hot", [P, TOP_K, 4, NR])
        row_f = sb("row_f", [P, TOP_K * 4])
        row_u = [sb(f"row_u{i}", [P, TOP_K * 4], U32) for i in range(2)]
        gsum = sb("gsum", [P, NC])
        gden = sb("gden", [P, NC])
        pick_v = sb("pick_v", [P, NC, TOP_K])
        hid = [sb(f"hid{i}", [P, W]) for i in range(2 * (NE - NR) * HB - 1)]
        dt_raw, dt_s, dt_p, dt_q = (hid[i][:, 0:NC * NH].rearrange("p (c h) -> p c h", h=NH) for i in range(4))
        banks = [ctx.enter_context(nc.psum_tensor(f"bank{i}", [P, BANK], F32)) for i in range(8)]

        act_banks, dve_banks = Ring(banks[0:3]), Ring(banks[3:6])
        proj_bank, down_bank = banks[6], banks[7]
        bank_free = {"proj": (), "down": ()}

        GROUPS = SLOT_TILES // 4
        spare = xT[:]
        def carve(n):
            nonlocal spare
            got, spare = spare[:, 0:n], spare[:, n:]
            return got
        slots_in = [carve(4 * ROW).rearrange("p (n d) -> p n d", n=4) for _ in range(5)]
        slotsT = [carve(W) for _ in range(2)]
        w1_now = [carve(HB * P) for _ in range(4)]
        slots_out = [carve(W) for _ in range(3)]
        hidden_r = [hid[i][:] for i in range(4)]
        spare = xT[:]
        picked = [carve(TOP_K * W).rearrange("p (k c d) -> p k c d", k=TOP_K, c=4) for n in range(4)]

        def load(q, dst, src, signal):
            return q.put(lambda e: e.dma_start(dst, src), signal=signal, by=16)

        w1_v = w1_d.rearrange("p (e f) -> p e f", e=NE)
        w2_v = w2_d.rearrange("p (e k f) -> p e k f", e=NE, k=HB)
        xT_in = [None] * NB
        x_in = [None] * NB
        w_in_in = load(sp, w_in[:], w_in_d, "w_in_loaded")
        span = CPB * P
        xT_in[0] = load(sp, xT[:, 0:span], xT_d[:, 0:span], "xT0_loaded")
        params = [load(act, t if n == "router" else t[:], d, f"{n}_loaded") for n, t, d in (
            ("dt_bias", dt_bias, dt_bias_d), ("a_log", a_log, a_log_d), ("d_skip", d_skip, d_skip_d),
            ("conv_w", conv_w, conv_w_d), ("conv_b", conv_b, conv_b_d), ("norm_w", norm_w, norm_w_d),
            ("w_out", w_out, w_out_d), ("router", router[:, 0:NR], router_d), ("rms_w", rms_w, rms_w_d))]
        (dt_bias_in, a_log_in, d_skip_in, conv_w_in, conv_b_in, norm_w_in, w_out_in, router_in,
         rms_w_in) = params
        for b in range(NB):
            if b:
                xT_in[b] = load(sp, xT[:, b * span:(b + 1) * span], xT_d[:, b * span:(b + 1) * span],
                                f"xT{b}_loaded")
            x_in[b] = load(sp, x[:, b * CPB:(b + 1) * CPB, :], x_d[:, b * CPB:(b + 1) * CPB, :],
                           f"x{b}_loaded")
            if b == 1:
                w1_in = load(sp, w1_shared[:], w1_v[:, NR:], "w1_loaded")
                w2_in = load(sp, w2_shared[:], w2_v[:, NR:], "w2_loaded")

        def const(make, after=()):
            return pool.put(make, after=after, signal="consts")
        m1 = const(lambda e: e.memset(ones[:], 1.0))
        const(lambda e: e.memset(neg_half[:], -0.5))
        router_pad = const(lambda e: e.memset(router[:, NR:], 0.0))
        for buf in xdt:
            const(lambda e, buf=buf: e.memset(buf[:, DI:], 0.0))
        for buf in chosen:
            const(lambda e, buf=buf: e.memset(buf[:, 4, :], 0.0))
        const(lambda e: e.affine_select(out=upto[:], in_=ones[:], compare_op=ALU.is_ge, fill=0.0, base=0,
                                        pattern=[[1, P]], channel_multiplier=-1), [m1])
        const(lambda e: e.affine_select(out=beyond[:], in_=ones[:], compare_op=ALU.is_gt, fill=0.0, base=0,
                                        pattern=[[-1, P]], channel_multiplier=1))
        const(lambda e: e.affine_select(out=before_b[:], in_=ones[:], compare_op=ALU.is_gt, fill=0.0, base=0,
                                        pattern=[[1, P]], channel_multiplier=-1))
        const(lambda e: e.affine_select(out=ident[:], in_=ones[:], compare_op=ALU.is_equal, fill=0.0, base=0,
                                        pattern=[[1, P]], channel_multiplier=-1))
        const(lambda e: e.memset(filler[:, 0:D], 0.0))
        const(lambda e: e.iota(filler[:, D:ROW].bitcast(I32), pattern=[[0, 1]], base=NOWHERE, channel_multiplier=0))
        iota_done = const(lambda e: e.iota(expert_no_i[:], pattern=[[1, NR]], base=0, channel_multiplier=0))
        expert_no_done = const(lambda e: e.tensor_copy(expert_no[:], expert_no_i[:]), [iota_done])
        iota_done = const(lambda e: e.iota(expert_no_i[:], pattern=[[0, NR]], base=0, channel_multiplier=1), [expert_no_done])
        consts = const(lambda e: e.tensor_copy(first_row[:], expert_no_i[:]), [iota_done])
        c1 = dve.put(lambda e: e.tensor_copy(ones_b[:], ones[:]), [consts], "consts_cast")
        c2 = dve.put(lambda e: e.tensor_copy(beyond_r[:], beyond[:]), [consts], "consts_cast")
        next_row_at = dve.put(lambda e: e.tensor_scalar(next_row[0][:], expert_no[:], float(REGION), None, ALU.mult), [consts], "consts_cast")
        filler_region = sp.put(lambda e: e.dma_start(dispatched[NR * REGION:NR * REGION + P, :], filler[:]), [consts], "filler_region", 16)

        for k in range(DI // P):
            w_out_ready = dve.put(lambda e, k=k: e.tensor_scalar(w_out[:, k, :], w_out[:, k, :], norm_w[:, k:k + 1], None, ALU.mult),
                                  [w_out_in, norm_w_in], "w_out_scaled")
        neg_rate = act.put(lambda e: e.activation(a_rate[:], a_log[:], ACT.Exp), [a_log_in], "rate")
        rate = dve.put(lambda e: e.tensor_scalar(a_rate[:], a_rate[:], -1.0, None, ALU.mult), [neg_rate], "rate_negated")

        def wide(ap, n):
            return ap.unsqueeze(len(ap.shape)).to_broadcast(list(ap.shape) + [n])

        def steps_of(c0, c1):
            n = c1 - c0
            bias = dt_bias[:].unsqueeze(1).to_broadcast([P, 4, NH])
            for q0 in range(c0, c1, 4):
                i, bank, free = dve_banks.take()
                for c in range(q0, q0 + 4):
                    made = pe.put(lambda e, c=c, bank=bank: e.matmul(bank[:, c % 4 * P:(c % 4 + 1) * P], xT[:, c * P:(c + 1) * P],
                                                                     w_in[:, w_in.shape[1] - P:], start=True, stop=True),
                                  [w_in_in, xT_in[c // CPB], *free], "dt_raw")
                d = dve.put(lambda e, q0=q0, bank=bank: e.tensor_tensor(dt_raw[:, q0:q0 + 4, :], bank[:].rearrange("p (c f) -> p c f", c=4)[:, :, P - NH:], bias, ALU.add),
                            [made, dt_bias_in], "dt")
                dve_banks.free[i] = (d,)
            cut = slice(c0, c1)
            v, s, p, q, t = (a[:, cut, :] for a in (dt_raw, dt_s, dt_p, dt_q, dt))
            d = dve.put(lambda e: e.scalar_tensor_tensor(q, v, -1.0, v, ALU.mult, ALU.min), [d], "dt")
            a = act.put(lambda e: e.activation(s, q, ACT.Exp), [d], "dt_exp")
            d = dve.put(lambda e: e.tensor_scalar(q, s, 2.0, None, ALU.add), [a], "dt")
            d = dve.put(lambda e: e.reciprocal(q, q), [d], "dt")
            d = dve.put(lambda e: e.tensor_tensor(s, s, q, ALU.mult), [d], "dt")
            d = dve.put(lambda e: e.tensor_tensor(q, s, s, ALU.mult), [d], "dt")
            d = dve.put(lambda e: e.tensor_scalar(p, q, 1.0 / (2 * LOG1P_TERMS + 1), None, ALU.mult), [d], "dt")
            for k in range(LOG1P_TERMS - 1, 0, -1):
                d = dve.put(lambda e, k=k: e.scalar_tensor_tensor(p, p, 1.0 / (2 * k + 1), q, ALU.add, ALU.mult), [d], "dt")
            d = dve.put(lambda e: e.scalar_tensor_tensor(p, p, 1.0, s, ALU.add, ALU.mult), [d], "dt")
            d = dve.put(lambda e: e.tensor_scalar(v, v, 0.0, None, ALU.max), [d], "dt")
            d = dve.put(lambda e: e.scalar_tensor_tensor(t, p, 2.0, v, ALU.mult, ALU.add), [d], "dt")
            al = a_log_step[:, cut, :]
            rates = a_rate[:].unsqueeze(1).to_broadcast([P, n, NH])
            d = dve.put(lambda e: e.tensor_tensor(al, t, rates, ALU.mult), [d, rate], "dt")
            d = dve.put(lambda e: e.tensor_scalar(al, al, A_FLOOR, None, ALU.max), [d], "dt")
            d = dve.put(lambda e: e.tensor_copy(a_hi[:, cut, :], al), [d], "dt")
            d = dve.put(lambda e: e.tensor_tensor(a_lo[:, cut, :], al, a_hi[:, cut, :].bitcast(F32), ALU.subtract), [d], "dt")
            for lhs, dst in ((upto, into), (beyond, outof), (ones, whole)):
                i, bank, free = act_banks.take()
                s_ps = bank[:, 0:n * NH]
                m = pe.put(lambda e, lhs=lhs, s_ps=s_ps: e.matmul(s_ps, lhs[:], a_log_step[:, cut, :].rearrange("p c h -> p (c h)"), start=True, stop=True),
                           [d, consts, *free], "chunk_sums")
                a = act.put(lambda e, dst=dst, s_ps=s_ps: e.activation(dst[:, cut, :].rearrange("p c h -> p (c h)"), s_ps, ACT.Exp), [m], "chunk_decays")
                act_banks.free[i] = (a,)
            return d, a

        arow_free = [None, None]
        decay_free = [None] * len(decay)

        def decays_of(c, steps):
            bufs, slot = arow[c % 2], c % len(decay)
            for buf, part in zip(bufs, (a_hi, a_lo)):
                one = pool.put(lambda e, buf=buf, part=part: e.tensor_tensor(buf[:], upto[:].unsqueeze(1).to_broadcast([P, NH, P]),
                                                                             part[:, c, :].bitcast(F32).unsqueeze(2).to_broadcast([P, NH, P]), ALU.mult),
                               [steps[0], consts, arow_free[c % 2]], "arow")
            i, bank, free = act_banks.take()
            for n, buf in enumerate(bufs):
                m = pe.put(lambda e, n=n, buf=buf: e.matmul(bank[:], beyond_r[:], buf[:].rearrange("p h i -> p (h i)"), start=(n == 0), stop=(n == 1)),
                           [one, c2, *free], "segment_sums")
            arow_free[c % 2] = m
            a = act.put(lambda e: e.activation(decay[slot].rearrange("p h i -> p (h i)"), bank[:], ACT.Exp),
                        [m, decay_free[slot]], "decays")
            act_banks.free[i] = (a,)
            return a

        raw_free = {}
        tail_done = {}
        xbc_done = {}
        xbc_read = {}

        def conv_of(u):
            t, k = divmod(u, NBLK)
            b, r, o = t // TPB, raw[u % len(raw)], xbcT[t % 2]
            free_r = raw_free.get(u - len(raw), ())
            if t % TPB == 0:
                halo = pool.put(lambda e: e.memset(r[:, 0:TAPS - 1], 0.0), free_r, "halo")
            else:
                halo = pool.put(lambda e: e.tensor_copy(r[:, 0:TAPS - 1], tail[:, k, :]), [*free_r, tail_done[k]], "halo")
            i, bank, free = act_banks.take()
            m = pe.put(lambda e: e.matmul(bank[:], w_in[:, DI + k * P:DI + (k + 1) * P], xT[:, t * W:(t + 1) * W], start=True, stop=True),
                       [xT_in[b], w_in_in, *free], "xbc")
            a = act.put(lambda e: e.activation(r[:, TAPS - 1:], bank[:], ACT.Copy), [m, *free_r], "xbc_raw")
            tail_done[k] = pool.put(lambda e: e.tensor_copy(tail[:, k, :], r[:, W:W + TAPS - 1]), [a, halo], "tail")
            a = act.put(lambda e: e.activation(o[:, k, :], bank[:], ACT.Identity, scale=conv_w[:, k, 0:1], bias=conv_b[:, k:k + 1]),
                        [conv_w_in, conv_b_in, xbc_read.get((t - 2, k))], "xbc_raw")
            act_banks.free[i] = (a,)
            d = a
            for n in range(TAPS - 1):
                d = dve.put(lambda e, n=n: e.scalar_tensor_tensor(o[:, k, :], r[:, n:n + W], conv_w[:, k, TAPS - 1 - n:TAPS - n], o[:, k, :], ALU.mult, ALU.add),
                            [d, halo], "conv")
            raw_free[u] = (d, tail_done[k])
            xbc_done[t, k] = act.put(lambda e: e.activation(o[:, k, :], o[:, k, :], ACT.Silu), [d], "xbc_silu")

        zs_free = [None] * len(zs)

        def z_of(c):
            i, bank, free = act_banks.take()
            s = c % len(zs)
            m = pe.put(lambda e: e.matmul(bank[:, 0:DI], xT[:, c * P:(c + 1) * P], w_in[:, 0:DI], start=True, stop=True),
                       [xT_in[c // CPB], w_in_in, *free], "z")
            a = act.put(lambda e: e.activation(zs[s][:], bank[:, 0:DI], ACT.Silu), [m, zs_free[s]], "z_silu")
            act_banks.free[i] = (a,)
            return a

        free_xb, free_gram, free_mix, free_xdt, free_xend, free_xskip, free_y = ([()] * 2 for _ in range(7))
        state_done = {}
        state_read = {}
        g_free = [()] * len(g)
        heads = lambda ap: ap.rearrange("p (h e) -> p h e", h=NH)
        per_head = lambda s: s.unsqueeze(2).to_broadcast([P, NH, HD])

        def sum_squares(dst, src, after):
            i, buf, free = squares.take()
            a = act.put(lambda e: e.activation(buf[:, 0:src.shape[1]], src, ACT.Square, accum_out=dst), [after, *free], "squares")
            squares.free[i] = (a,)
            return a

        def scan_turn(c):
            t, at, h = c // 4, (c % 4) * P, c % 2
            o = xbcT[t % 2]
            i, bank, free = act_banks.take()
            for k in range(3):
                m = pe.put(lambda e, k=k: e.transpose(bank[:, k * P:(k + 1) * P], o[:, k, at:at + P], ident[:]), [xbc_done[t, k], consts, *free], "token_major")
            a = act.put(lambda e: e.activation(xb[h][:], bank[:, 0:3 * P], ACT.Copy), [m, *free_xb[h]], "xb")
            act_banks.free[i] = (a,)
            xv = heads(xb[h][:, 0:DI])
            p1 = dve.put(lambda e: e.tensor_tensor(heads(xdt[h][:, 0:DI]), xv, per_head(dt[:, c, :]), ALU.mult), [a, consts, *free_xdt[h]], "xdt")
            p2 = dve.put(lambda e: e.tensor_tensor(heads(xend[h][:]), heads(xdt[h][:, 0:DI]), per_head(outof[:, c, :]), ALU.mult), [p1, *free_xend[h]], "xend")
            free_xb[h] = (p1,)
            if c % 4 == 3:
                for k in range(2):
                    xbc_read[t, k] = m
            return dict(xdt=p1, xend=p2, xb=a)

        def scan_pe(c, made):
            i, bank, free = dve_banks.take()
            gram_at = slice(DI, DI + P)
            after = None
            if c < NC:
                t, at, h = c // 4, (c % 4) * P, c % 2
                o = xbcT[t % 2]
                mg = pe.put(lambda e: e.matmul(bank[:, gram_at], o[:, 2, at:at + P], o[:, 3, at:at + P], start=True, stop=True), [xbc_done[t, 2], xbc_done[t, 3], *free], "gram")
                if c % 4 == 3:
                    xbc_read[t, 2] = mg
                dgm = dve.put(lambda e: e.tensor_tensor(gram[h][:], bank[:, gram_at], upto[:], ALU.mult), [mg, *free_gram[h], consts], "gram_masked") if c == 0 else None
            if c == 0:
                dve_banks.free[i] = (dgm,)
            else:
                p, ph = made[c - 1], (c - 1) % 2
                mu = pe.put(lambda e: e.matmul(bank[:, 0:DI], xb[ph][:, DI:DI + P], xend[ph][:], start=True, stop=True), [p["xend"], p["xb"], *free], "state_add")
                free_xend[ph] = (mu,)
                free_xb[ph] = (*free_xb[ph], mu)
                first = (c - 1) % CPB == 0
                before = state_read.get(c - 3, ())
                if first:
                    ds = dve.put(lambda e: e.tensor_copy(state[(c - 1) % 2][:], bank[:, 0:DI]), [mu, *before], "state")
                else:
                    pk = pool.put(lambda e: e.tensor_tensor(heads(state_kept[:]), heads(state[c % 2][:]), per_head(whole[:, c - 1, :]), ALU.mult), [state_done[c - 2]], "state_kept")
                    ds = dve.put(lambda e: e.tensor_tensor(state[(c - 1) % 2][:], bank[:, 0:DI], state_kept[:], ALU.add), [mu, pk, *before], "state")
                    state_read[c - 2] = (*state_read.get(c - 2, ()), pk)
                state_done[c - 1] = ds
                if c < NC:
                    dgm = dve.put(lambda e: e.tensor_tensor(gram[h][:], bank[:, gram_at], upto[:], ALU.mult), [mg, *free_gram[h]], "gram_masked")
                    dve_banks.free[i] = (ds, dgm)
                else:
                    dve_banks.free[i] = (ds,)
            if c < NC:
                slot = c % len(decay)
                dm = dve.put(lambda e: e.tensor_tensor(mix[h][:], decay[slot], gram[h][:].unsqueeze(1).to_broadcast([P, NH, P]), ALU.mult),
                             [dec[c], dgm, *free_mix[h]], "mix")
                decay_free[slot] = dm
                free_gram[h] = (dm,)
                made[c]["mix"] = dm

        def scan_out(c, made, z):
            p, t, at, h = made[c], c // 4, (c % 4) * P, c % 2
            o = xbcT[t % 2]
            first = c % CPB == 0
            iy, ybank, yfree = dve_banks.take()
            for k in range(NH):
                my = pe.put(lambda e, k=k: e.matmul(ybank[:, k * HD:k * HD + P], mix[h][:, k, :], xdt[h][:, k * HD:k * HD + P], start=True, stop=True),
                            [p["mix"], p["xdt"], *yfree], "y_inside")
            if not first:
                my = pe.put(lambda e: e.matmul(ybank[:, DI:2 * DI], o[:, 3, at:at + P], state[(c - 1) % 2][:], start=True, stop=True), [state_done[c - 1]], "y_carried")
                state_read[c - 1] = (my,)
            if c % 4 == 3:
                xbc_read[t, 3] = my
            free_mix[h] = (my,)
            free_xdt[h] = (my, p["xend"])
            y = y_inside if first else y_carried
            px = dve.put(lambda e: e.tensor_tensor(heads(xskip[:]), heads(xb[h][:, 0:DI]), per_head(d_skip[:]), ALU.mult), [d_skip_in, p["xb"], *free_xskip[0]], "xskip")
            free_xb[h] = (*free_xb[h], px)
            if not first:
                dve.put(lambda e: e.tensor_tensor(heads(y_carried[:]), heads(ybank[:, DI:2 * DI]), per_head(into[:, c, :]), ALU.mult), [my, *free_y[0]], "y")
            dy = dve.put(lambda e: e.tensor_tensor(y_inside[:], ybank[:, 0:DI], xskip[:], ALU.add), [my, px, *free_y[0]], "y")
            dve_banks.free[iy] = (dy,)
            free_xskip[0] = (dy,)
            if not first:
                dy = dve.put(lambda e: e.tensor_tensor(y_carried[:], y_carried[:], y_inside[:], ALU.add), [dy], "y")
            gi, zi = c % len(g), c % len(zs)
            dg = dve.put(lambda e: e.tensor_tensor(g[gi][:], y[:], zs[zi][:], ALU.mult), [dy, z, *g_free[gi]], "gated")
            zs_free[zi] = dg
            free_y[0] = (dg,)
            a = sum_squares(g_ss[:, c:c + 1], g[gi][:], dg)
            return dg, a

        gT_free = [None, None]
        gT_done = {}

        def pow_of(dst, src, mul, add, after, signal, keep=None):
            base = dst if keep is None else keep
            one = pool.put(lambda e: e.tensor_scalar(base, src, mul, add, ALU.mult, ALU.add), after, signal)
            return pool.put(lambda e: e.tensor_tensor(dst, base, neg_half[:, 0:src.shape[1]], ALU.pow), [one], signal)

        def turn_g(c, gated):
            gi = c % len(g)
            i, bank, free = act_banks.take()
            for k in range(DI // P):
                m = pe.put(lambda e, k=k: e.transpose(bank[:, k * P:(k + 1) * P], g[gi][:, k * P:(k + 1) * P], ident[:]), [gated[c][0], *free], "gT")
            g_free[gi] = (m, gated[c][1])
            a = act.put(lambda e: e.activation(gT[c % 2][:].rearrange("p k i -> p (k i)"), bank[:, 0:DI], ACT.Copy), [m, gT_free[c % 2]], "gT_copied")
            act_banks.free[i] = (a,)
            gT_done[c] = a

        def project(c, gated):
            j = c % 4
            for k in range(DI // P):
                m = pe.put(lambda e, k=k: e.matmul(proj_bank[:, j * D:(j + 1) * D], gT[c % 2][:, k, :], w_out[:, k, :], start=(k == 0), stop=(k == DI // P - 1)),
                           [gT_done[c], w_out_ready, *bank_free["proj"]], "out_proj")
            gT_free[c % 2] = m
            if j < 3:
                return None
            c0 = c - 3
            rs = pow_of(g_rs[:, c0:c0 + 4], g_ss[:, c0:c0 + 4], 1.0 / DI, LN_EPS, [gated[c][1]], "g_rs")
            for n in range(4):
                d = dve.put(lambda e, n=n: e.scalar_tensor_tensor(x[:, c0 + n, :], proj_bank[:, n * D:(n + 1) * D], g_rs[:, c0 + n:c0 + n + 1], x[:, c0 + n, :], ALU.mult, ALU.add), [m, rs, x_in[c // CPB]], "residual")
            bank_free["proj"] = (d,)
            return ln_stats(c // 4, d)

        def ln_stats(t, after):
            for c in range(4 * t, 4 * t + 4):
                d = dve.put(lambda e, c=c: e.bn_stats(bn[:, c, :], x[:, c, :]), [after], "ln_stats")
            for c in range(4 * t, 4 * t + 4):
                d = dve.put(lambda e, c=c: e.bn_aggr(mv[:, c, :], bn[:, c, :]), [d], "ln_stats")
            return d

        def normalise(t, stats, signal):
            c0 = 4 * t
            r = pow_of(rstd[:, c0:c0 + 4], mv[:, c0:c0 + 4, 1], 1.0, LN_EPS, [stats], signal + "_rstd")
            for c in range(c0, c0 + 4):
                d = dve.put(lambda e, c=c: e.tensor_scalar(x[:, c, :], x[:, c, :], mv[:, c, 0:1], rstd[:, c:c + 1], ALU.subtract, ALU.mult), [r, stats], signal)
            return d

        rows_free = [(), ()]
        xn_done, rq_done, expert_in, logits_done, last_scatter = {}, {}, {}, {}, {}
        xnT_free = [()] * len(xnT)

        def feed(t, stats):
            c0, cut = 4 * t, slice(4 * t, 4 * t + 4)
            d = normalise(t, stats, "x1")
            for c in range(c0, c0 + 4):
                a = sum_squares(x_ss[:, c:c + 1], x[:, c, :], d)
            rs = pow_of(x_rs[:, cut], x_ss[:, cut], 1.0 / D, RMS_EPS, [a], "x_rs", keep=x_ms[:, cut])
            rq_done[t] = dve.put(lambda e: e.tensor_tensor(x_rq[:, cut], x_ms[:, cut], x_rs[:, cut], ALU.mult), [rs], "x_rq")
            buf = rows[t % 2]
            target = pool.put(lambda e: e.iota(buf[:, :, :, D:ROW].bitcast(I32).rearrange("p k c o -> p k (c o)"), pattern=[[TOK, TOP_K], [P, 4]], base=c0 * P, channel_multiplier=1), rows_free[t % 2], "row_targets")
            for k in range(TOP_K):
                for c in range(c0, c0 + 4):
                    a = act.put(lambda e, k=k, c=c: e.activation(buf[:, k, c - c0, 0:D], x[:, c, :], ACT.Copy, scale=x_rs[:, c:c + 1]), [rs, *rows_free[t % 2]], "xn")
                if k == 0:
                    xn_done[t] = a
            last_scatter[t] = [a, target]

        def turn_x(t):
            i, bank, free = act_banks.take()
            for k in range(4):
                m = pe.put(lambda e, k=k: e.transpose(bank[:, k * P:(k + 1) * P], rows[t % 2][:, 0, k, 0:D], ident[:]), [xn_done[t], *free], "xnT")
            a = act.put(lambda e: e.activation(xnT[t % 3][:], bank[:], ACT.Copy), [m, *xnT_free[t % 3]], "xnT_copied")
            act_banks.free[i] = (a,)
            rows_free[t % 2] = (m,)
            expert_in[t] = a

        def route(t):
            c0, cut = 4 * t, slice(4 * t, 4 * t + 4)
            i, bank, free = dve_banks.take()
            for k in range(4):
                m = pe.put(lambda e, k=k: e.matmul(bank[:, k * P:(k + 1) * P], xnT[t % 3][:, k * P:(k + 1) * P], router[:], start=True, stop=True), [expert_in[t], router_in, consts, *free], "router")
            dl = dve.put(lambda e: e.tensor_tensor(logits[:, cut, :], bank[:].rearrange("p (c r) -> p c r", c=4)[:, :, 0:NR], x_rq[:, cut].unsqueeze(2).to_broadcast([P, 4, NR]), ALU.mult), [m, rq_done[t]], "logits")
            dve_banks.free[i] = (dl,)
            xnT_free[t % 3] = (m,)
            for c in range(4):
                d = dve.put(lambda e, c=c: e.max(top_v[:, c0 + c, :], logits[:, c0 + c, :]), [dl], "top")
            for c in range(4):
                d = dve.put(lambda e, c=c: e.max_index(top_i[:, c, :], top_v[:, c0 + c, :], logits[:, c0 + c, :]), [d, row_seen[0]], "top")
            d = dve.put(lambda e: e.tensor_copy(top_f[:], top_i[:, :, 0:TOP_K]), [d], "top")
            for k in range(TOP_K):
                d = dve.put(lambda e, k=k: e.tensor_tensor(hot[:, k], expert_no[:].unsqueeze(1).to_broadcast([P, 4, NR]), top_f[:, :, k:k + 1].to_broadcast([P, 4, NR]), ALU.is_equal), [d, consts], "hot")
            ch = chosen[t % 2]
            logits_done[t] = dve.put(lambda e: e.tensor_tensor(ch[:, 0:4, :], hot[:, 0], hot[:, 1], ALU.add), [d, ranked[0]], "hot")

        row_seen = [None]
        ranked = [None]
        next_done = [next_row_at]
        row_u_free = [(), ()]

        def dispatch(t):
            i, bank, free = dve_banks.take()
            ch, n5 = chosen[t % 2], 5 * NR
            pe.put(lambda e: e.matmul(bank[:, 0:n5], before_b[:], ch[:].rearrange("p c r -> p (c r)"), start=True, stop=False, skip_group_check=True), [logits_done[t], c1, *free], "rank")
            for c in range(4):
                m = pe.put(lambda e, c=c: e.matmul(bank[:, (c + 1) * NR:n5].rearrange("p (n r) -> p n r", r=NR), ones_b[:], ch[:, c:c + 1, :].to_broadcast([P, 4 - c, NR]), start=False, stop=(c == 3), skip_group_check=True), [], "rank")
            ranked[0] = m
            now, then = next_row[t % 2], next_row[(t + 1) % 2]
            d = dve.put(lambda e: e.tensor_tensor(row_of[:], bank[:, 0:4 * NR].rearrange("p (c r) -> p c r", r=NR), now[:].unsqueeze(1).to_broadcast([P, 4, NR]), ALU.add), [m, next_done[0], row_seen[0]], "rows")
            dn = dve.put(lambda e: e.tensor_tensor(then[:], bank[:, 4 * NR:n5], now[:], ALU.add), [m, row_seen[0]], "rows")
            dve_banks.free[i] = (dn,)
            next_done[0] = dn
            for k in range(TOP_K):
                d2 = dve.put(lambda e, k=k: e.tensor_tensor(row_hot[:, k], hot[:, k], row_of[:], ALU.mult), [d, row_seen[0]], "rows")
            d = dve.put(lambda e: e.tensor_reduce(row_f[:], row_hot[:].rearrange("p k c r -> p (k c) r"), AX.X, ALU.add), [d2], "rows")
            d = dve.put(lambda e: e.tensor_copy(row_u[t % 2][:], row_f[:]), [d, *row_u_free[t % 2]], "rows")
            row_seen[0] = d
            for k in range(TOP_K):
                for c in range(4):
                    s = pool.put(lambda e, k=k, c=c: e.indirect_dma_start(dispatched, bass.IndirectOffsetOnAxis(ap=row_u[t % 2][:, 4 * k + c:4 * k + c + 1], axis=0), rows[t % 2][:, k, c, :], None),
                                 [d, *last_scatter[t]], f"dispatched{t % 2}", 16)
            rows_free[t % 2] = (*rows_free[t % 2], s)
            row_u_free[t % 2] = (s,)
            last_scatter[t] = s

        hid_free = [()] * len(hid)
        hid_done = {}
        acc_done = {}

        def scale_w1(w1, nos, loaded):
            for n, k in enumerate(nos):
                made = dve.put(lambda e, n=n, k=k: e.tensor_scalar(w1[:, n], w1[:, n], rms_w[:, k:k + 1], None, ALU.mult), [loaded, rms_w_in], "w1_scaled")
            return made

        def shared_hidden(t, u):
            e_no, k = divmod(u, HB)
            h = (4 * t + u) % len(hid)
            i, bank, free = act_banks.take()
            m = pe.put(lambda e: e.matmul(bank[:], w1_shared[:, e_no, k * P:(k + 1) * P], xnT[t % 3][:], start=True, stop=True),
                       [w1s_ready, expert_in[t], *free], "hidden")
            a = act.put(lambda e: e.activation(hid[h][:], bank[:], ACT.Silu), [m, *hid_free[h]], "hidden_silu")
            act_banks.free[i] = (a,)
            hid_done[t] = a
            if u == (NE - NR) * HB - 1:
                xnT_free[t % 3] = (*xnT_free[t % 3], m)

        def shared_down(t, c):
            n = (NE - NR) * HB
            for u in range(n):
                e_no, k = divmod(u, HB)
                m = pe.put(lambda e, u=u, e_no=e_no, k=k: e.matmul(down_bank[:, c * P:(c + 1) * P], hid[(4 * t + u) % len(hid)][:, c * P:(c + 1) * P], w2_shared[:, e_no, k, :], start=(u == 0), stop=(u == n - 1)),
                           [hid_done[t], w2_in, *bank_free["down"]], "down")
            if c == 3:
                for u in range(n):
                    hid_free[(4 * t + u) % len(hid)] = (m,)
                acc_done[t] = dve.put(lambda e: e.tensor_tensor(x[:, 4 * t:4 * t + 4, :], down_bank[:].rearrange("p (c d) -> p c d", c=4), x[:, 4 * t:4 * t + 4, :], ALU.add), [m, *last_xn[t]], "shared_added")
                bank_free["down"] = (acc_done[t],)

        def gate_weights():
            best = top_v[:, :, 0:1]
            d = dve.put(lambda e: e.tensor_tensor(gexp[:], logits[:], best.to_broadcast([P, NC, NR]), ALU.subtract), [logits_done[NT - 1]], "gate")
            d = dve.put(lambda e: e.tensor_tensor(pick_v[:], top_v[:, :, 0:TOP_K], best.to_broadcast([P, NC, TOP_K]), ALU.subtract), [], "gate")
            a = act.put(lambda e: e.activation(gexp[:], gexp[:], ACT.Exp), [d], "gate_exp")
            a = act.put(lambda e: e.activation(pick_v[:], pick_v[:], ACT.Exp), [], "gate_exp")
            d = dve.put(lambda e: e.tensor_reduce(gsum[:], gexp[:], AX.X, ALU.add), [a], "gate")
            d = dve.put(lambda e: e.reciprocal(gsum[:], gsum[:]), [d], "gate")
            d = dve.put(lambda e: e.tensor_tensor(pick_v[:], pick_v[:], gsum[:].unsqueeze(2).to_broadcast([P, NC, TOP_K]), ALU.mult), [d], "gate")
            d = dve.put(lambda e: e.tensor_reduce(gden[:], pick_v[:], AX.X, ALU.add), [d], "gate")
            d = dve.put(lambda e: e.tensor_scalar(gden[:], gden[:], GATE_EPS, None, ALU.add), [d], "gate")
            d = dve.put(lambda e: e.reciprocal(gden[:], gden[:]), [d], "gate")
            return dve.put(lambda e: e.tensor_tensor(pick_v[:], pick_v[:], gden[:].unsqueeze(2).to_broadcast([P, NC, TOP_K]), ALU.mult), [d], "gate")

        TP = SLOT_TILES // 8
        end_row = sb("end_row", [P, NR])
        fill_row = sb("fill_row", [P, NR], U32)
        count_i = sb("count_i", [P, NR], I32)
        tiles_of = sb("tiles_of", [P, NR])
        lower = sb("lower", [P, NR, NR])
        tile_base = sb("tile_base", [P, NR])
        tile_end = sb("tile_end", [P, NR])
        tile_no = sb("tile_no", [TP, 8])
        tile_no_i = sb("tile_no_i", [TP, 8], I32)
        is_past = sb("is_past", [TP, 8, NR])
        is_in = sb("is_in", [TP, 8, NR])
        in_any = sb("in_any", [TP, 8])
        t_expert = sb("t_expert", [TP, 8])
        t_row = sb("t_row", [TP, 8])
        row_base = sb("row_base", [TP, NR])
        expert_reg = sb("expert_reg", [TP, 8], I32)
        row_reg = sb("row_reg", [TP, 8], I32)

        def tables():
            now = next_row[NT % 2]
            d0 = dve.put(lambda e: e.tensor_tensor(fill_row[:], now[:], first_row[:], ALU.add), [next_done[0]], "table")
            for n in range(NR):
                filled = pool.put(lambda e, n=n: e.indirect_dma_start(dispatched, bass.IndirectOffsetOnAxis(ap=fill_row[:, n:n + 1], axis=0), filler[:], None), [d0], "filled", 16)
            d = dve.put(lambda e: e.scalar_tensor_tensor(end_row[:], expert_no[:], -float(REGION), now[:], ALU.mult, ALU.add), [d0], "table")
            d = dve.put(lambda e: e.tensor_scalar(count_i[:], end_row[:], float(P - 1), None, ALU.add), [d], "table")
            d = dve.put(lambda e: e.tensor_scalar(count_i[:], count_i[:], P.bit_length() - 1, None, ALU.arith_shift_right), [d], "table")
            d = dve.put(lambda e: e.tensor_copy(tiles_of[:], count_i[:]), [d], "table")
            d = dve.put(lambda e: e.tensor_tensor(lower[:], expert_no[:].unsqueeze(1).to_broadcast([P, NR, NR]), expert_no[:].unsqueeze(2).to_broadcast([P, NR, NR]), ALU.is_lt), [d], "table")
            d = dve.put(lambda e: e.tensor_tensor(lower[:], lower[:], tiles_of[:].unsqueeze(1).to_broadcast([P, NR, NR]), ALU.mult), [d], "table")
            d = dve.put(lambda e: e.tensor_reduce(tile_base[:], lower[:], AX.X, ALU.add), [d], "table")
            d = dve.put(lambda e: e.tensor_tensor(tile_end[:], tile_base[:], tiles_of[:], ALU.add), [d], "table")
            d = dve.put(lambda e: e.tensor_scalar(row_base[:], tile_base[0:TP, :], -float(P), None, ALU.mult), [d], "table")
            d = dve.put(lambda e: e.scalar_tensor_tensor(row_base[:], expert_no[0:TP, :], float(REGION), row_base[:], ALU.mult, ALU.add), [d], "table")
            tn = tile_no[:].unsqueeze(2).to_broadcast([TP, 8, NR])
            by_tile = lambda a: a.unsqueeze(1).to_broadcast([TP, 8, NR])
            d = dve.put(lambda e: e.tensor_tensor(is_past[:], tn, by_tile(tile_end[0:TP, :]), ALU.is_ge), [d, tile_no_done], "table")
            d = dve.put(lambda e: e.tensor_tensor(is_in[:], tn, by_tile(tile_base[0:TP, :]), ALU.is_ge), [d], "table")
            d = dve.put(lambda e: e.tensor_tensor(is_in[:], is_in[:], is_past[:], ALU.subtract), [d], "table")
            d = dve.put(lambda e: e.tensor_reduce(in_any[:], is_in[:], AX.X, ALU.add), [d], "table")
            d = dve.put(lambda e: e.tensor_reduce(t_expert[:], is_past[:], AX.X, ALU.add), [d], "table")
            ex = dve.put(lambda e: e.tensor_scalar(expert_reg[:], t_expert[:], float(NR - 1), None, ALU.min), [d], "table")
            d = dve.put(lambda e: e.tensor_tensor(is_in[:], is_in[:], by_tile(row_base[:]), ALU.mult), [ex], "table")
            d = dve.put(lambda e: e.tensor_reduce(t_row[:], is_in[:], AX.X, ALU.add), [d], "table")
            d = dve.put(lambda e: e.scalar_tensor_tensor(t_expert[:], tile_no[:], float(P), in_any[:], ALU.mult, ALU.mult), [d], "table")
            d = dve.put(lambda e: e.tensor_tensor(t_row[:], t_row[:], t_expert[:], ALU.add), [d], "table")
            d = dve.put(lambda e: e.tensor_scalar(in_any[:], in_any[:], -float(NR * REGION), float(NR * REGION), ALU.mult, ALU.add), [d], "table")
            d = dve.put(lambda e: e.tensor_tensor(row_reg[:], t_row[:], in_any[:], ALU.add), [d], "table")
            return filled, ex, d

        regs = {}

        def load_regs(q, engine, name, table, n, after):
            def make(e):
                hi = NR - 1 if name == "expert" else NR * REGION
                _, vals = nc.values_load_multi_w_load_instructions(table[n // 8:n // 8 + 1, 0:8], engines=(engine,), min_val=0, max_val=hi, skip_runtime_bounds_check_because="worked out from counts")
                for j, v in enumerate(vals):
                    regs[q.name, n + j] = v
            q.put(make, [after])

        slots_free = [()] * len(slots_in)
        slots_done = {}
        slotsT_free, slotsT_done = [()] * 2, {}
        w1_free, w1_done = [()] * len(w1_now), {}
        hr_free, hr_done = [()] * len(hidden_r), {}
        out_free = [()] * len(slots_out)

        def fetch(gr, tab):
            if gr % 2 == 0:
                load_regs(sp, ET.SP, "row", row_reg, 4 * gr, tab[2])
            b = gr % len(slots_in)
            for n in range(4):
                s = sp.put(lambda e, n=n: e.dma_start(slots_in[b][:, n, :], dispatched[bass.ds(regs["sp", 4 * gr + n], P), :]),
                           [*slots_free[b], *slots_ready], f"slots_in{b}", 16)
            slots_done[gr] = s

        def turn_slots(gr):
            b = gr % len(slots_in)
            i, bank, free = dve_banks.take()
            for n in range(4):
                m = pe.put(lambda e, n=n: e.transpose(bank[:, n * P:(n + 1) * P], slots_in[b][:, n, 0:D], ident[:]), [slots_done[gr], *free], "slotsT")
            d = dve.put(lambda e: e.tensor_copy(slotsT[gr % 2], bank[:]), [m, *slotsT_free[gr % 2]], "slotsT_copied")
            dve_banks.free[i] = (d,)
            slots_free[b] = (m,)
            slotsT_done[gr] = d

        def pick_w1(n, tab):
            if n % 8 == 0:
                load_regs(dve, ET.DVE, "expert", expert_reg, n, tab[1])
            b = n % len(w1_now)
            w1_done[n] = dve.put(lambda e: e.tensor_copy(w1_now[b], w1_routed[:, bass.ds(regs["dve", n], 1), :].rearrange("p o f -> p (o f)")), [w1r_ready[0], *w1_free[b]], "w1_picked")

        def routed_hidden(n2):
            i, bank, free = act_banks.take()
            for n in (2 * n2, 2 * n2 + 1):
                gr, b = n // 4, n % len(w1_now)
                for k in range(HB):
                    at = (n % 2 * HB + k) * P
                    m = pe.put(lambda e, at=at, k=k, b=b, gr=gr, n=n: e.matmul(bank[:, at:at + P], w1_now[b][:, k * P:(k + 1) * P], slotsT[gr % 2][:, n % 4 * P:(n % 4 + 1) * P], start=True, stop=True),
                               [w1_done[n], slotsT_done[gr], *free], "routed_hidden")
                w1_free[b] = (m,)
            if n % 4 == 3:
                slotsT_free[gr % 2] = (m,)
            hb = n2 % len(hidden_r)
            hr_done[n2] = act.put(lambda e: e.activation(hidden_r[hb], bank[:], ACT.Silu), [m, *hr_free[hb]], "routed_silu")
            act_banks.free[i] = (hr_done[n2],)

        def routed_down(gr, tab):
            if gr % 2 == 0:
                load_regs(pe, ET.PE, "expert", expert_reg, 4 * gr, tab[1])
            i, bank, free = dve_banks.take()
            for n in range(4 * gr, 4 * gr + 4):
                n2, j = n // 2, n % 4
                hb = n2 % len(hidden_r)
                for k in range(HB):
                    at = (n % 2 * HB + k) * P
                    m = pe.put(lambda e, n=n, k=k, at=at, hb=hb, j=j: e.matmul(bank[:, j * P:(j + 1) * P], hidden_r[hb][:, at:at + P], w2_routed[:, bass.ds(regs["pe", n], 1), k * D:(k + 1) * D].rearrange("p o f -> p (o f)"), start=(k == 0), stop=(k == HB - 1)),
                               [hr_done[n2], w2r_in[0], *free], "routed_down")
                hr_free[hb] = (m,)
            b, sb_ = gr % len(slots_out), gr % len(slots_in)
            d = dve.put(lambda e: e.tensor_copy(slots_out[b], bank[:]), [m, *out_free[b]], "routed_out")
            dve_banks.free[i] = (d,)
            for n in range(4):
                s = pool.put(lambda e, n=n: e.indirect_dma_start(returned, bass.IndirectOffsetOnAxis(ap=slots_in[sb_][:, n, D:ROW].bitcast(U32), axis=0), slots_out[b][:, n * P:(n + 1) * P], None, bounds_check=NOWHERE - 1, oob_is_err=False),
                             [d], f"returned{b}", 16)
            out_free[b] = (s,)
            slots_free[sb_] = (*slots_free[sb_], s)
            return s

        picked_free = [()] * len(picked)
        picked_done = {}

        def gather(t, done):
            b = t % len(picked)
            for k in range(TOP_K):
                src = returned[k * TOK + t * W:k * TOK + (t + 1) * W, :].rearrange("(c p) d -> p c d", p=P)
                s = sp.put(lambda e, k=k, src=src: e.dma_start(picked[b][:, k], src), [*done, *picked_free[b]], f"picked{b}", 16)
            picked_done[t] = s

        def finish(t, gate):
            b = t % len(picked)
            for k in range(TOP_K):
                for c in range(4 * t, 4 * t + 4):
                    d = dve.put(lambda e, c=c, k=k: e.scalar_tensor_tensor(x[:, c, :], picked[b][:, k, c % 4, :], pick_v[:, c, k:k + 1], x[:, c, :], ALU.mult, ALU.add),
                                [picked_done[t], gate, acc_done[t], d if k else None], "routed_added")
            picked_free[b] = (d,)
            d = ln_stats(t, d)
            return d

        def store(t, d):
            d = normalise(t, d, "x2")
            return sp.put(lambda e: e.dma_start(out_d[:, 4 * t:4 * t + 4, :], x[:, 4 * t:4 * t + 4, :]), [d], "stored", 16)

        tile_no_done = pool.put(lambda e: e.iota(tile_no_i[:], pattern=[[1, 8]], base=0, channel_multiplier=8), [], "consts")
        tile_no_done = pool.put(lambda e: e.tensor_copy(tile_no[:], tile_no_i[:]), [tile_no_done], "consts")
        head = steps_of(0, CPB)
        dec = {c: decays_of(c, head) for c in range(CPB)}
        rest = steps_of(CPB, NC)
        w1s_ready = scale_w1(w1_shared, range(NR, NE), w1_in)
        w1r_ready, w2r_in, last_xn = [None], [None], {}
        for u in range(5):
            conv_of(u)
        zt, made, gated, stats = {0: z_of(0)}, {}, {}, {}
        for i in range(NC + 22):
            if i < NC:
                made[i] = scan_turn(i)
            if i <= NC:
                scan_pe(i, made)
            if i < NC and i + 5 < NT * NBLK:
                conv_of(i + 5)
            if i + 1 < NC:
                zt[i + 1] = z_of(i + 1)
            if 1 <= i <= NC:
                gated[i - 1] = scan_out(i - 1, made, zt[i - 1])
            if 3 <= i < NC + 3:
                turn_g(i - 3, gated)
            if 4 <= i < NC + 4:
                got = project(i - 4, gated)
                if got is not None:
                    stats[(i - 4) // 4] = got
            j, k = i - 8, i % 4
            t = j // 4
            if k == 0 and 0 <= t < NT:
                feed(t, stats[t])
                last_xn[t] = list(last_scatter[t])
            if k == 1 and 0 <= t < NT:
                turn_x(t)
            if k == 2 and 0 <= t < NT:
                route(t)
            if k == 3 and 0 <= t < NT:
                dispatch(t)
            u = i - 14
            if 0 <= u < 4 * NT:
                shared_down(u // 4, u % 4)
            u = i - 10
            if 0 <= u < 4 * NT:
                shared_hidden(u // 4, u % 4)
            if i % CPB == CPB - 2 and i + 2 < NC:
                b = i // CPB + 1
                for n in range(b * CPB, (b + 1) * CPB):
                    dec[n] = decays_of(n, rest)
            if i == NC + 1:
                w2r_in[0] = sp.put(lambda e: e.dma_start(w2_routed, w2_d[:, 0:NR * HB * D].rearrange("p (e f) -> p e f", e=NR)), [xbc_read[t, n] for n in range(NBLK) for t in (NT - 2, NT - 1)], "w2r_loaded", 16)
                w1r_in = sp.put(lambda e: e.dma_start(w1_routed, w1_v[:, 0:NR]), decay_free, "w1r_loaded", 16)
            if i == NC + 7:
                w1r_ready[0] = scale_w1(w1_routed, range(NR), w1r_in)
            if i == 4 * (NT - 1) + 11:
                tab = tables()
                slots_ready = (last_scatter[NT - 1], last_scatter[NT - 2], tab[0], filler_region)
        gate = gate_weights()
        for gr in range(4):
            fetch(gr, tab)
        turn_slots(0)
        for n in range(4):
            pick_w1(n, tab)
        routed_hidden(0)
        routed_hidden(1)
        tails = {}
        for gr in range(GROUPS):
            if gr + 1 < GROUPS:
                turn_slots(gr + 1)
                for n in range(4):
                    pick_w1(4 * (gr + 1) + n, tab)
                routed_hidden(2 * gr + 2)
                routed_hidden(2 * gr + 3)
            tails[gr % len(slots_out)] = routed_down(gr, tab)
            if gr + 4 < GROUPS:
                fetch(gr + 4, tab)
        done = list(tails.values())
        for t in range(3):
            gather(t, done)
        got = {}
        for t in range(NT + 1):
            if t + 3 < NT:
                gather(t + 3, done)
            if t < NT:
                got[t] = finish(t, gate)
            if t:
                last = store(t - 1, got[t - 1])
        sp.put(lambda e: e.nop(), [last])

        semaphores = {n: ctx.enter_context(nc.semaphore(n)) for n in counts}
        block = ctx.enter_context(nc.Block())

        @block.sync
        def _(e):
            sp.play(e, semaphores)

        @block.scalar
        def _(e):
            act.play(e, semaphores)

        @block.vector
        def _(e):
            dve.play(e, semaphores)

        @block.gpsimd
        def _(e):
            pool.play(e, semaphores)

        @block.tensor
        def _(e):
            pe.play(e, semaphores)


def kernel(**inputs):
    import numpy as np
    import concourse.bacc as bacc
    from concourse.bass_utils import run_bass_kernel_spmd

    a = {n: np.asarray(v) for n, v in inputs.items()}
    x = a["L0_attn_x"]
    nb, length, d = x.shape
    tokens = x.reshape(nb * length, d)
    chunks = tokens.shape[0] // P

    def channels(v, n=P):
        return np.moveaxis(v.reshape(*v.shape[:-1], -1, n), -1, 0)

    def rows(v):
        return np.broadcast_to(v[None], (P, *v.shape))

    w1 = np.concatenate([a["L0_ffn_w1"], a["L0_ffn_w1_s"]])
    w2 = np.concatenate([a["L0_ffn_w2"], a["L0_ffn_w2_s"]])
    rms = np.concatenate([a["L0_ffn_rms_w"], a["L0_ffn_rms_w_s"]])
    arrays = {
        "xT": tokens.T,
        "x": tokens.reshape(chunks, P, d).transpose(1, 0, 2),
        "w_in": a["L0_attn_in_proj_w"],
        "conv_w": channels(a["L0_attn_conv_w"]).transpose(0, 2, 1),
        "conv_b": channels(a["L0_attn_conv_b"]),
        "norm_w": channels(a["L0_attn_norm_w"]),
        "w_out": a["L0_attn_out_proj_w"].reshape(-1, P, d).transpose(1, 0, 2),
        "dt_bias": rows(a["L0_attn_dt_bias"]),
        "a_log": rows(a["L0_attn_A_log"]),
        "d_skip": rows(a["L0_attn_D"]),
        "router": a["L0_ffn_router_w"],
        "rms_w": rms.T,
        "w1": w1.transpose(1, 0, 2).reshape(d, -1),
        "w2": w2.reshape(w2.shape[0], -1, P, d).transpose(2, 0, 1, 3).reshape(P, -1),
    }
    arrays = {n: np.ascontiguousarray(v) for n, v in arrays.items()}
    nc = bacc.Bacc("TRN2", target_bir_lowering=False, num_devices=1)
    args = [nc.dram_tensor(n + "_dram", v.shape, F32, kind="ExternalInput").ap() for n, v in arrays.items()]
    out = nc.dram_tensor("out_dram", (P, chunks, d), F32, kind="ExternalOutput").ap()
    mamba_moe(nc, *args, out)
    r = run_bass_kernel_spmd(nc, [{n + "_dram": v for n, v in arrays.items()}], core_ids=[0])
    got = r.results[0]["out_dram"]
    return np.ascontiguousarray(got.transpose(1, 0, 2)).reshape(nb, length, d)
```

```python
from contextlib import ExitStack

import concourse.bass as bass
from concourse import mybir

F32 = mybir.dt.float32
F32R = mybir.dt.float32r
BF16 = mybir.dt.bfloat16
I32 = mybir.dt.int32
U32 = mybir.dt.uint32
ET = mybir.EngineType
ALU = mybir.AluOpType
ACT = mybir.ActivationFunctionType
AX = mybir.AxisListType
P = 128
BANK = 512
TAPS = 4
TOP_K = 2
LN_EPS = 1e-5
RMS_EPS = 1.1920929e-07
GATE_EPS = 1e-9
A_FLOOR = -200.0
LOG1P_TERMS = 8


class Queue:

    def __init__(self, name, counts):
        self.name, self.steps, self.seen, self.counts = name, [], {}, counts

    def put(self, make, after=(), signal=None, by=1):
        waits = []
        for done in after:
            if done is not None and self.seen.get(done[0], 0) < done[1]:
                self.seen[done[0]] = done[1]
                waits.append(done)
        token = None
        if signal is not None:
            self.counts[signal] = self.counts.get(signal, 0) + by
            token = (signal, self.counts[signal])
        self.steps.append((waits, make, signal, by))
        return token

    def play(self, engine, semaphores):
        for waits, make, signal, by in self.steps:
            for name, value in waits:
                engine.wait_ge(semaphores[name], value)
            made = make(engine)
            if signal is not None:
                made.then_inc(semaphores[signal], by)


class Ring:

    def __init__(self, buffers):
        self.buffers, self.free, self.at = buffers, [()] * len(buffers), -1

    def take(self):
        self.at = (self.at + 1) % len(self.buffers)
        free, self.free[self.at] = self.free[self.at], None
        assert free is not None, "its reader is not queued yet"
        return self.at, self.buffers[self.at], free


def mamba_moe(nc, xT_d, x_d, w_in_d, conv_w_d, conv_b_d, norm_w_d, w_out_d, dt_bias_d, a_log_d,
              d_skip_d, router_d, rms_w_d, w1_d, w2_d, out_d):
    D = xT_d.shape[0]
    TOK = xT_d.shape[1]
    NB = 8
    NC = TOK // P
    CPB = NC // NB
    NT = NC // 4
    TPB = NT // NB
    NH = dt_bias_d.shape[1]
    DI = norm_w_d.shape[1] * P
    HD = DI // NH
    NBLK = conv_b_d.shape[1]
    NE = w1_d.shape[1] // (2 * P)
    NR = router_d.shape[1]
    HB = 2
    W = 4 * P
    REGION = TOK + P
    SLOT_TILES = -(-(TOP_K * TOK // P + NR - 1) // 8) * 8
    NOWHERE = TOP_K * TOK
    dispatched = nc.dram_tensor("dispatched", [(NR + 1) * REGION, D + 1], F32, kind="Internal").ap()
    returned = nc.dram_tensor("returned", [TOP_K * TOK, D], F32, kind="Internal").ap()

    counts = {}
    pe, act, dve, pool, sp = (Queue(n, counts) for n in ("pe", "act", "dve", "pool", "sp"))

    with ExitStack() as ctx:
        def sb(name, shape, dt=F32):
            return ctx.enter_context(nc.sbuf_tensor(name, shape, dt))

        xT = sb("xT", [P, TOK])
        x = sb("x", [P, NC, D])
        w_in = sb("w_in", [P, w_in_d.shape[1]])
        conv_w = sb("conv_w", [P, NBLK, TAPS])
        conv_b = sb("conv_b", [P, NBLK])
        norm_w = sb("norm_w", [P, DI // P])
        w_out = sb("w_out", [P, DI // P, D])
        dt_bias = sb("dt_bias", [P, NH])
        a_log = sb("a_log", [P, NH])
        d_skip = sb("d_skip", [P, NH])
        router = sb("router", [P, P])
        rms_w = sb("rms_w", [P, NE])
        w1_shared = sb("w1_shared", [P, NE - NR, HB * P])
        w2_shared = sb("w2_shared", [P, NE - NR, HB, D])
        ident = sb("ident", [P, P])
        upto = sb("upto", [P, P])
        beyond = sb("beyond", [P, P])
        beyond_r = sb("beyond_r", [P, P], F32R)
        before_b = sb("before_b", [P, P], BF16)
        ones = sb("ones", [P, P])
        ones_b = sb("ones_b", [P, P], BF16)
        neg_half = sb("neg_half", [P, 8])
        expert_no = sb("expert_no", [P, NR])
        expert_no_i = sb("expert_no_i", [P, NR], I32)
        a_rate = sb("a_rate", [P, NH])
        dt = sb("dt", [P, NC, NH])
        a_log_step = sb("a_log_step", [P, NC, NH])
        a_hi = sb("a_hi", [P, NC, NH], F32R)
        a_lo = sb("a_lo", [P, NC, NH], F32R)
        into = sb("into", [P, NC, NH])
        outof = sb("outof", [P, NC, NH])
        whole = sb("whole", [P, NC, NH])
        arow_area = sb("arow_area", [P, 5, 2, NH, P], F32R)
        arow = [[arow_area[:, i, n] for n in range(2)] for i in range(5)]
        decay_area = sb("decay_area", [P, 7, NH, P])
        decay = [decay_area[:, i] for i in range(7)]
        w1_routed = decay_area[:].rearrange("p n h i -> p (n h i)")[:, 0:NR * HB * P].rearrange("p (e f) -> p e f", e=NR)
        raw = [sb(f"raw{i}", [P, TAPS - 1 + W]) for i in range(3)]
        tail = sb("tail", [P, NBLK, TAPS - 1])
        xbcT_area = sb("xbcT_area", [P, 2, NBLK, W])
        xbcT = [xbcT_area[:, i] for i in range(2)]
        w2_routed = xbcT_area[:].rearrange("p n k i -> p (n k i)")[:, 0:NR * HB * D].rearrange("p (e f) -> p e f", e=NR)
        zs = [sb(f"zs{i}", [P, DI]) for i in range(3)]
        xb = [sb(f"xb{i}", [P, DI + P]) for i in range(4)]
        gram = [sb(f"gram{i}", [P, P]) for i in range(2)]
        mix = [sb(f"mix{i}", [P, NH, P]) for i in range(2)]
        xdt = [sb(f"xdt{i}", [P, DI + HD]) for i in range(2)]
        xend = [sb(f"xend{i}", [P, DI]) for i in range(2)]
        xskip = sb("xskip", [P, DI])
        state = [sb(f"state{i}", [P, DI]) for i in range(2)]
        state_kept = sb("state_kept", [P, DI])
        y_carried = sb("y_carried", [P, DI])
        y_inside = sb("y_inside", [P, DI])
        g = [sb(f"g{i}", [P, DI]) for i in range(2)]
        squares = Ring([sb(f"squares{i}", [P, DI], BF16) for i in range(2)])
        g_ss = sb("g_ss", [P, NC])
        g_rs = sb("g_rs", [P, NC])
        gT = [sb(f"gT{i}", [P, DI // P, P]) for i in range(2)]
        bn = sb("bn", [P, NC, 6])
        mv = sb("mv", [P, NC, 2])
        rstd = sb("rstd", [P, NC])
        x_ss = sb("x_ss", [P, NC])
        x_ms = sb("x_ms", [P, NC])
        x_rs = sb("x_rs", [P, NC])
        x_rq = sb("x_rq", [P, NC])
        ROW = D + 1
        rows = [sb(f"rows{i}", [P, TOP_K, 4, ROW]) for i in range(3)]
        filler = sb("filler", [P, ROW])
        xnT = [xT[:, t * W:(t + 1) * W] for t in range(NT)]
        logits = sb("logits", [P, NC, NR])
        top_v = sb("top_v", [P, NC, 8])
        top_i = sb("top_i", [P, 4, 8], U32)
        top_f = sb("top_f", [P, 4, TOP_K])
        hot = sb("hot", [P, TOP_K, 4, NR])
        chosen = [sb(f"chosen{i}", [P, 5, NR], BF16) for i in range(2)]
        next_row = [sb(f"next_row{i}", [P, NR]) for i in range(2)]
        row_of = sb("row_of", [P, 4, NR])
        row_hot = sb("row_hot", [P, TOP_K, 4, NR])
        row_f = sb("row_f", [P, TOP_K * 4])
        row_u = [sb(f"row_u{i}", [P, TOP_K * 4], U32) for i in range(2)]
        gsum = sb("gsum", [P, NC])
        gden = sb("gden", [P, NC])
        pick_v = sb("pick_v", [P, NC, TOP_K])
        hid = [sb(f"hid{i}", [P, W]) for i in range(2 * (NE - NR) * HB - 1)]
        dt_raw, dt_s, dt_p, dt_q = (hid[i][:, 0:NC * NH].rearrange("p (c h) -> p c h", h=NH) for i in range(4))
        banks = [ctx.enter_context(nc.psum_tensor(f"bank{i}", [P, BANK], F32)) for i in range(8)]

        act_banks, dve_banks = Ring(banks[0:3]), Ring(banks[3:6])
        proj_bank, down_bank = banks[6], banks[7]
        bank_free = {"proj": (), "down": ()}

        GROUPS = SLOT_TILES // 4
        spare = arow_area[:].rearrange("p b n h i -> p (b n h i)").bitcast(F32)
        def carve(n):
            nonlocal spare
            got, spare = spare[:, 0:n], spare[:, n:]
            return got
        slots_in = [carve(4 * ROW).rearrange("p (n d) -> p n d", n=4) for _ in range(9)]
        spare = xT[:]
        slots_out = [carve(W) for _ in range(3)]
        slotsT = [carve(W) for _ in range(3)]
        w1_now = [carve(HB * P) for _ in range(8)]
        gexp = carve(NC * NR).rearrange("p (c r) -> p c r", c=NC)
        AREA_UNITS = 4 * -(-(TOK - spare.shape[1]) // W)
        hidden_r = [hid[i][:] for i in range(4)]
        spare = xT[:]
        picked = [carve(TOP_K * W).rearrange("p (k c d) -> p k c d", k=TOP_K, c=4) for n in range(6)]

        def load(q, dst, src, signal):
            return q.put(lambda e: e.dma_start(dst, src), signal=signal, by=16)

        w1_v = w1_d.rearrange("p (e f) -> p e f", e=NE)
        w2_v = w2_d.rearrange("p (e k f) -> p e k f", e=NE, k=HB)
        xT_in = [None] * NB
        x_in = [None] * NB
        w_in_in = load(sp, w_in[:], w_in_d, "w_in_loaded")
        span = CPB * P
        xT_in[0] = load(sp, xT[:, 0:span], xT_d[:, 0:span], "xT0_loaded")
        params = [load(act, t if n == "router" else t[:], d, f"{n}_loaded") for n, t, d in (
            ("dt_bias", dt_bias, dt_bias_d), ("a_log", a_log, a_log_d), ("d_skip", d_skip, d_skip_d),
            ("conv_w", conv_w, conv_w_d), ("conv_b", conv_b, conv_b_d), ("norm_w", norm_w, norm_w_d),
            ("w_out", w_out, w_out_d), ("router", router[:, 0:NR], router_d), ("rms_w", rms_w, rms_w_d))]
        (dt_bias_in, a_log_in, d_skip_in, conv_w_in, conv_b_in, norm_w_in, w_out_in, router_in,
         rms_w_in) = params
        for b in range(NB):
            if b:
                xT_in[b] = load(sp, xT[:, b * span:(b + 1) * span], xT_d[:, b * span:(b + 1) * span],
                                f"xT{b}_loaded")
            x_in[b] = load(sp, x[:, b * CPB:(b + 1) * CPB, :], x_d[:, b * CPB:(b + 1) * CPB, :],
                           f"x{b}_loaded")
            if b == 1:
                w1_in = load(sp, w1_shared[:], w1_v[:, NR:], "w1_loaded")
                w2_in = load(sp, w2_shared[:], w2_v[:, NR:], "w2_loaded")

        def const(make, after=()):
            return pool.put(make, after=after, signal="consts")
        m1 = const(lambda e: e.memset(ones[:], 1.0))
        const(lambda e: e.memset(neg_half[:], -0.5))
        router_pad = const(lambda e: e.memset(router[:, NR:], 0.0))
        for buf in xdt:
            const(lambda e, buf=buf: e.memset(buf[:, DI:], 0.0))
        for buf in chosen:
            const(lambda e, buf=buf: e.memset(buf[:, 4, :], 0.0))
        const(lambda e: e.affine_select(out=upto[:], in_=ones[:], compare_op=ALU.is_ge, fill=0.0, base=0,
                                        pattern=[[1, P]], channel_multiplier=-1), [m1])
        const(lambda e: e.affine_select(out=beyond[:], in_=ones[:], compare_op=ALU.is_gt, fill=0.0, base=0,
                                        pattern=[[-1, P]], channel_multiplier=1))
        const(lambda e: e.affine_select(out=before_b[:], in_=ones[:], compare_op=ALU.is_gt, fill=0.0, base=0,
                                        pattern=[[1, P]], channel_multiplier=-1))
        const(lambda e: e.affine_select(out=ident[:], in_=ones[:], compare_op=ALU.is_equal, fill=0.0, base=0,
                                        pattern=[[1, P]], channel_multiplier=-1))
        const(lambda e: e.memset(filler[:, 0:D], 0.0))
        const(lambda e: e.iota(filler[:, D:ROW].bitcast(I32), pattern=[[0, 1]], base=NOWHERE, channel_multiplier=0))
        iota_done = const(lambda e: e.iota(expert_no_i[:], pattern=[[1, NR]], base=0, channel_multiplier=0))
        consts = const(lambda e: e.tensor_copy(expert_no[:], expert_no_i[:]), [iota_done])
        c1 = dve.put(lambda e: e.tensor_copy(ones_b[:], ones[:]), [consts], "consts_cast")
        c2 = dve.put(lambda e: e.tensor_copy(beyond_r[:], beyond[:]), [consts], "consts_cast")
        next_row_at = dve.put(lambda e: e.tensor_scalar(next_row[0][:], expert_no[:], float(REGION), None, ALU.mult), [consts], "consts_cast")
        filler_region = sp.put(lambda e: e.dma_start(dispatched[NR * REGION:NR * REGION + P, :], filler[:]), [consts], "filler_region", 16)

        for k in range(DI // P):
            w_out_ready = dve.put(lambda e, k=k: e.tensor_scalar(w_out[:, k, :], w_out[:, k, :], norm_w[:, k:k + 1], None, ALU.mult),
                                  [w_out_in, norm_w_in], "w_out_scaled")
        neg_rate = act.put(lambda e: e.activation(a_rate[:], a_log[:], ACT.Exp), [a_log_in], "rate")
        rate = dve.put(lambda e: e.tensor_scalar(a_rate[:], a_rate[:], -1.0, None, ALU.mult), [neg_rate], "rate_negated")

        def wide(ap, n):
            return ap.unsqueeze(len(ap.shape)).to_broadcast(list(ap.shape) + [n])

        log_decays_done, chunk_decays_done = {}, {}

        def steps_of(c0, c1):
            n = c1 - c0
            bias = dt_bias[:].unsqueeze(1).to_broadcast([P, 4, NH])
            for q0 in range(c0, c1, 4):
                i, bank, free = act_banks.take()
                for c in range(q0, q0 + 4):
                    made = pe.put(lambda e, c=c, bank=bank: e.matmul(bank[:, c % 4 * P:(c % 4 + 1) * P], xT[:, c * P:(c + 1) * P],
                                                                     w_in[:, w_in.shape[1] - P:], start=True, stop=True),
                                  [w_in_in, xT_in[c // CPB], *free], "dt_raw")
                d = dve.put(lambda e, q0=q0, bank=bank: e.tensor_tensor(dt_raw[:, q0:q0 + 4, :], bank[:].rearrange("p (c f) -> p c f", c=4)[:, :, P - NH:], bias, ALU.add),
                            [made, dt_bias_in], "dt")
                act_banks.free[i] = (d,)
            cut = slice(c0, c1)
            v, s, p, q, t = (a[:, cut, :] for a in (dt_raw, dt_s, dt_p, dt_q, dt))
            d = dve.put(lambda e: e.scalar_tensor_tensor(q, v, -1.0, v, ALU.mult, ALU.min), [d], "dt")
            yield
            a = act.put(lambda e: e.activation(s, q, ACT.Exp), [d], "dt_exp")
            yield
            d = dve.put(lambda e: e.tensor_scalar(q, s, 2.0, None, ALU.add), [a], "dt")
            yield
            d = dve.put(lambda e: e.reciprocal(q, q), [d], "dt")
            yield
            d = dve.put(lambda e: e.tensor_tensor(s, s, q, ALU.mult), [d], "dt")
            yield
            d = dve.put(lambda e: e.tensor_tensor(q, s, s, ALU.mult), [d], "dt")
            yield
            d = dve.put(lambda e: e.tensor_scalar(p, q, 1.0 / (2 * LOG1P_TERMS + 1), None, ALU.mult), [d], "dt")
            yield
            for k in range(LOG1P_TERMS - 1, 0, -1):
                d = dve.put(lambda e, k=k: e.scalar_tensor_tensor(p, p, 1.0 / (2 * k + 1), q, ALU.add, ALU.mult), [d], "dt")
                yield
            d = dve.put(lambda e: e.scalar_tensor_tensor(p, p, 1.0, s, ALU.add, ALU.mult), [d], "dt")
            yield
            d = dve.put(lambda e: e.tensor_scalar(v, v, 0.0, None, ALU.max), [d], "dt")
            yield
            d = dve.put(lambda e: e.scalar_tensor_tensor(t, p, 2.0, v, ALU.mult, ALU.add), [d], "dt")
            yield
            al = a_log_step[:, cut, :]
            rates = a_rate[:].unsqueeze(1).to_broadcast([P, n, NH])
            d = dve.put(lambda e: e.tensor_tensor(al, t, rates, ALU.mult), [d, rate], "dt")
            yield
            d = dve.put(lambda e: e.tensor_scalar(al, al, A_FLOOR, None, ALU.max), [d], "dt")
            yield
            d = dve.put(lambda e: e.tensor_copy(a_hi[:, cut, :], al), [d], "dt")
            yield
            d = dve.put(lambda e: e.tensor_tensor(a_lo[:, cut, :], al, a_hi[:, cut, :].bitcast(F32), ALU.subtract), [d], "dt")
            yield
            for c in range(c0, c1):
                log_decays_done[c] = d
            yield
            for lhs, dst in ((upto, into), (beyond, outof), (ones, whole)):
                i, bank, free = act_banks.take()
                s_ps = bank[:, 0:n * NH]
                m = pe.put(lambda e, lhs=lhs, s_ps=s_ps: e.matmul(s_ps, lhs[:], a_log_step[:, cut, :].rearrange("p c h -> p (c h)"), start=True, stop=True),
                           [d, consts, *free], "chunk_sums")
                a = act.put(lambda e, dst=dst, s_ps=s_ps: e.activation(dst[:, cut, :].rearrange("p c h -> p (c h)"), s_ps, ACT.Exp), [m], "chunk_decays")
                act_banks.free[i] = (a,)
            for c in range(c0, c1):
                chunk_decays_done[c] = a
            yield

        arow_free = [None] * len(arow)
        decay_free = [None] * len(decay)
        arow_done = {}

        def arows_of(c):
            for buf, part in zip(arow[c % len(arow)], (a_hi, a_lo)):
                arow_done[c] = pool.put(lambda e, buf=buf, part=part: e.tensor_tensor(buf, upto[:].unsqueeze(1).to_broadcast([P, NH, P]),
                                                                                      part[:, c, :].bitcast(F32).unsqueeze(2).to_broadcast([P, NH, P]), ALU.mult),
                                        [log_decays_done[c], consts, arow_free[c % len(arow)]], "arow")

        def decays_of(c):
            slot = c % len(decay)
            i, bank, free = act_banks.take()
            for n, buf in enumerate(arow[c % len(arow)]):
                m = pe.put(lambda e, n=n, buf=buf: e.matmul(bank[:], beyond_r[:], buf.rearrange("p h i -> p (h i)"), start=(n == 0), stop=(n == 1)),
                           [arow_done[c], c2, *free], "segment_sums")
            arow_free[c % len(arow)] = m
            a = act.put(lambda e: e.activation(decay[slot].rearrange("p h i -> p (h i)"), bank[:], ACT.Exp),
                        [m, decay_free[slot]], "decays")
            act_banks.free[i] = (a,)
            return a

        raw_free = {}
        tail_done = {}
        xbc_done = {}
        xbc_read = {}

        conv_in, conv_sum = {}, {}

        def conv_project(u):
            t, k = divmod(u, NBLK)
            b, r, o = t // TPB, raw[u % len(raw)], xbcT[t % 2]
            free_r = raw_free.get(u - len(raw), ())
            if t % TPB == 0:
                halo = pool.put(lambda e: e.memset(r[:, 0:TAPS - 1], 0.0), free_r, "halo")
            else:
                halo = pool.put(lambda e: e.tensor_copy(r[:, 0:TAPS - 1], tail[:, k, :]), [*free_r, tail_done[k]], "halo")
            i, bank, free = act_banks.take()
            m = pe.put(lambda e: e.matmul(bank[:], w_in[:, DI + k * P:DI + (k + 1) * P], xT[:, t * W:(t + 1) * W], start=True, stop=True),
                       [xT_in[b], w_in_in, *free], "xbc")
            a = act.put(lambda e: e.activation(r[:, TAPS - 1:], bank[:], ACT.Copy), [m, *free_r], "xbc_raw")
            a2 = act.put(lambda e: e.activation(o[:, k, :], bank[:], ACT.Identity, scale=conv_w[:, k, 0:1], bias=conv_b[:, k:k + 1]),
                         [conv_w_in, conv_b_in, xbc_read.get((t - 2, k))], "xbc_raw")
            act_banks.free[i] = (a2,)
            conv_in[u] = (a, a2, halo)

        def conv_taps(u):
            t, k = divmod(u, NBLK)
            r, o = raw[u % len(raw)], xbcT[t % 2]
            a, d, halo = conv_in[u]
            tail_done[k] = pool.put(lambda e: e.tensor_copy(tail[:, k, :], r[:, W:W + TAPS - 1]), [a, halo], "tail")
            for n in range(TAPS - 1):
                d = dve.put(lambda e, n=n: e.scalar_tensor_tensor(o[:, k, :], r[:, n:n + W], conv_w[:, k, TAPS - 1 - n:TAPS - n], o[:, k, :], ALU.mult, ALU.add),
                            [d, halo], "conv")
                yield
            raw_free[u] = (d, tail_done[k])
            conv_sum[u] = d

        def conv_silu(u):
            t, k = divmod(u, NBLK)
            o = xbcT[t % 2]
            xbc_done[t, k] = act.put(lambda e: e.activation(o[:, k, :], o[:, k, :], ACT.Silu), [conv_sum[u]], "xbc_silu")

        zs_free = [None] * len(zs)
        xT_read = {}

        def z_of(c):
            i, bank, free = act_banks.take()
            s = c % len(zs)
            m = pe.put(lambda e: e.matmul(bank[:, 0:DI], xT[:, c * P:(c + 1) * P], w_in[:, 0:DI], start=True, stop=True),
                       [xT_in[c // CPB], w_in_in, *free], "z")
            a = act.put(lambda e: e.activation(zs[s][:], bank[:, 0:DI], ACT.Silu), [m, zs_free[s]], "z_silu")
            act_banks.free[i] = (a,)
            xT_read[c // 4] = m
            return a

        free_gram, free_mix, free_xdt, free_xend = ([()] * 2 for _ in range(4))
        state_done = {}
        state_read = {}
        g_free = [()] * len(g)
        heads = lambda ap: ap.rearrange("p (h e) -> p h e", h=NH)
        per_head = lambda s: s.unsqueeze(2).to_broadcast([P, NH, HD])

        def sum_squares(dst, src, after):
            i, buf, free = squares.take()
            a = act.put(lambda e: e.activation(buf[:, 0:src.shape[1]], src, ACT.Square, accum_out=dst), [after, *free], "squares")
            squares.free[i] = (a,)
            return a

        chunk = {}

        def turn_xb(c):
            t, at = c // 4, (c % 4) * P
            o, buf = xbcT[t % 2], xb[c % len(xb)]
            i, bank, free = act_banks.take()
            for k in range(3):
                m = pe.put(lambda e, k=k: e.transpose(bank[:, k * P:(k + 1) * P], o[:, k, at:at + P], ident[:]), [xbc_done[t, k], consts, *free], "token_major")
            a = act.put(lambda e: e.activation(buf[:], bank[:, 0:3 * P], ACT.Copy), [m, *chunk.get(c - len(xb), {}).get("xb_free", ())], "xb")
            act_banks.free[i] = (a,)
            if c % 4 == 3:
                for k in range(2):
                    xbc_read[t, k] = m
            chunk[c] = dict(xb=a)

        def gram_and_state_add(c, cs):
            i, bank, free = dve_banks.take()
            if c < NC:
                t, at = c // 4, (c % 4) * P
                o = xbcT[t % 2]
                m = pe.put(lambda e: e.matmul(bank[:, DI:DI + P], o[:, 2, at:at + P], o[:, 3, at:at + P], start=True, stop=True), [xbc_done[t, 2], xbc_done[t, 3], *free], "gram")
                if c % 4 == 3:
                    xbc_read[t, 2] = m
                chunk[c]["gram"] = (bank, m, i)
            if cs >= 0:
                h, buf = cs % 2, xb[cs % len(xb)]
                m = pe.put(lambda e: e.matmul(bank[:, 0:DI], buf[:, DI:DI + P], xend[h][:], start=True, stop=True), [chunk[cs]["xend"], chunk[cs]["xb"], *free], "state_add")
                free_xend[h] = (m,)
                if c < NC:
                    chunk[c]["gram"] = (bank, m, i)
                chunk[cs]["xb_free"] = (*chunk[cs].get("xb_free", ()), m)
                chunk[cs]["add"] = (bank, m, i)

        def outputs(c):
            t, at, h = c // 4, (c % 4) * P, c % 2
            o = xbcT[t % 2]
            i, bank, free = dve_banks.take()
            for k in range(NH):
                m = pe.put(lambda e, k=k: e.matmul(bank[:, k * HD:k * HD + P], mix[h][:, k, :], xdt[h][:, k * HD:k * HD + P], start=True, stop=True),
                           [chunk[c]["mix"], chunk[c]["xdt"], *free], "y_inside")
            free_mix[h] = (m,)
            free_xdt[h] = (m, chunk[c]["xend"])
            if c % CPB:
                m = pe.put(lambda e: e.matmul(bank[:, DI:2 * DI], o[:, 3, at:at + P], state[(c - 1) % 2][:], start=True, stop=True), [state_done[c - 1]], "y_carried")
                state_read[c - 1] = (*state_read.get(c - 1, ()), m)
            if c % 4 == 3:
                xbc_read[t, 3] = m
            chunk[c]["out"] = (bank, m, i)

        def masked_gram(c):
            bank, m, i = chunk[c]["gram"]
            d = dve.put(lambda e: e.tensor_tensor(gram[c % 2][:], bank[:, DI:DI + P], upto[:], ALU.mult), [m, *free_gram[c % 2], consts], "gram_masked")
            chunk[c]["gram_masked"] = d
            dve_banks.free[i] = (d,)
            yield

        def next_state(c):
            bank, m, i = chunk[c]["add"]
            before = state_read.get(c - 2, ())
            if c % CPB == 0:
                d = dve.put(lambda e: e.tensor_copy(state[c % 2][:], bank[:, 0:DI]), [m, *before], "state")
            else:
                d = dve.put(lambda e: e.tensor_tensor(state[c % 2][:], bank[:, 0:DI], state_kept[:], ALU.add), [m, kept[c], *before], "state")
            state_done[c] = d
            dve_banks.free[i] = (d,)

        kept = {}

        def keep_state(c):
            if c % CPB:
                kept[c] = pool.put(lambda e: e.tensor_tensor(heads(state_kept[:]), heads(state[(c - 1) % 2][:]), per_head(whole[:, c, :]), ALU.mult), [state_done[c - 1], chunk_decays_done[c]], "state_kept")
                state_read[c - 1] = (*state_read.get(c - 1, ()), kept[c])

        def scale_x(c):
            h, xv = c % 2, heads(xb[c % len(xb)][:, 0:DI])
            d = dve.put(lambda e: e.tensor_tensor(heads(xdt[h][:, 0:DI]), xv, per_head(dt[:, c, :]), ALU.mult), [chunk[c]["xb"], consts, *free_xdt[h]], "xdt")
            chunk[c]["xdt"] = d
            yield
            chunk[c]["xend"] = dve.put(lambda e: e.tensor_tensor(heads(xend[h][:]), heads(xdt[h][:, 0:DI]), per_head(outof[:, c, :]), ALU.mult), [d, chunk_decays_done[c], *free_xend[h]], "xend")
            chunk[c]["xb_free"] = (d,)
            yield

        def mixing(c):
            slot, h = c % len(decay), c % 2
            d = dve.put(lambda e: e.tensor_tensor(mix[h][:], decay[slot], gram[h][:].unsqueeze(1).to_broadcast([P, NH, P]), ALU.mult),
                        [dec[c], chunk[c]["gram_masked"], *free_mix[h]], "mix")
            decay_free[slot] = d
            free_gram[h] = (d,)
            chunk[c]["mix"] = d
            yield

        def skip_x(c):
            px = pool.put(lambda e: e.tensor_tensor(heads(xskip[:]), heads(xb[c % len(xb)][:, 0:DI]), per_head(d_skip[:]), ALU.mult), [d_skip_in, chunk[c]["xb"], *free_xskip], "xskip")
            chunk[c]["xskip"] = px

        free_xskip = []

        def gram_then_mix(c):
            yield from masked_gram(c)
            yield from mixing(c)

        def gate_y(c):
            bank, m, i = chunk[c]["out"]
            px = chunk[c]["xskip"]
            chunk[c]["xb_free"] = (*chunk[c]["xb_free"], px)
            if c % CPB:
                dc = dve.put(lambda e: e.tensor_tensor(heads(y_carried[:]), heads(bank[:, DI:2 * DI]), per_head(into[:, c, :]), ALU.mult), [m, chunk_decays_done[c], gated.get(c - 1)], "y")
                yield
            d = dve.put(lambda e: e.tensor_tensor(y_inside[:], bank[:, 0:DI], xskip[:], ALU.add), [m, px, gated.get(c - 1)], "y")
            free_xskip[:] = [d]
            dve_banks.free[i] = (d,)
            yield
            if c % CPB:
                d = dve.put(lambda e: e.tensor_tensor(y_inside[:], y_carried[:], y_inside[:], ALU.add), [d], "y")
                yield
            gi, zi = c % len(g), c % len(zs)
            d = dve.put(lambda e: e.tensor_tensor(g[gi][:], y_inside[:], zs[zi][:], ALU.mult), [d, zt[c], *g_free[gi]], "gated")
            zs_free[zi] = d
            gated[c] = d
            yield

        gT_free = [None, None]
        gT_done = {}

        def pow_of(dst, src, mul, add, after, signal, keep=None):
            base = dst if keep is None else keep
            one = pool.put(lambda e: e.tensor_scalar(base, src, mul, add, ALU.mult, ALU.add), after, signal)
            return pool.put(lambda e: e.tensor_tensor(dst, base, neg_half[:, 0:src.shape[1]], ALU.pow), [one], signal)

        def turn_g(c):
            gi = c % len(g)
            chunk[c]["g_ss"] = sum_squares(g_ss[:, c:c + 1], g[gi][:], gated[c])
            i, bank, free = act_banks.take()
            for k in range(DI // P):
                m = pe.put(lambda e, k=k: e.transpose(bank[:, k * P:(k + 1) * P], g[gi][:, k * P:(k + 1) * P], ident[:]), [gated[c], *free], "gT")
            g_free[gi] = (m, chunk[c]["g_ss"])
            a = act.put(lambda e: e.activation(gT[c % 2][:].rearrange("p k i -> p (k i)"), bank[:, 0:DI], ACT.Copy), [m, gT_free[c % 2]], "gT_copied")
            act_banks.free[i] = (a,)
            gT_done[c] = a

        def project(c):
            j = c % 4
            for k in range(DI // P):
                m = pe.put(lambda e, k=k: e.matmul(proj_bank[:, j * D:(j + 1) * D], gT[c % 2][:, k, :], w_out[:, k, :], start=(k == 0), stop=(k == DI // P - 1)),
                           [gT_done[c], w_out_ready, *bank_free["proj"]], "out_proj")
            gT_free[c % 2] = m
            if j == 3:
                projected[c // 4] = m

        def g_factor(t):
            c = 4 * t + 3
            g_rs_done[t] = pow_of(g_rs[:, c - 3:c + 1], g_ss[:, c - 3:c + 1], 1.0 / DI, LN_EPS, [chunk[c]["g_ss"]], "g_rs")

        projected, g_rs_done, stats = {}, {}, {}

        def residual(t):
            c0, m, rs = 4 * t, projected[t], g_rs_done[t]
            for n in range(4):
                d = dve.put(lambda e, n=n: e.scalar_tensor_tensor(x[:, c0 + n, :], proj_bank[:, n * D:(n + 1) * D], g_rs[:, c0 + n:c0 + n + 1], x[:, c0 + n, :], ALU.mult, ALU.add), [m, rs, x_in[c0 // CPB]], "residual")
                yield
            bank_free["proj"] = (d,)
            yield from ln_stats(t, d)

        def ln_stats(t, after):
            for c in range(4 * t, 4 * t + 4):
                d = dve.put(lambda e, c=c: e.bn_stats(bn[:, c, :], x[:, c, :]), [after], "ln_stats")
                yield
            for c in range(4 * t, 4 * t + 4):
                d = dve.put(lambda e, c=c: e.bn_aggr(mv[:, c, :], bn[:, c, :]), [d], "ln_stats")
                yield
            stats[t] = d

        rstd_done = {}

        def ln_factor(t):
            c0 = 4 * t
            rstd_done[t] = pow_of(rstd[:, c0:c0 + 4], mv[:, c0:c0 + 4, 1], 1.0, LN_EPS, [stats[t]], "rstd")

        shift = sb("shift", [P, NC])
        shift_done = {}

        def ln_shift(t):
            shift_done[t] = dve.put(lambda e: e.scalar_tensor_tensor(shift[:, 4 * t:4 * t + 4], mv[:, 4 * t:4 * t + 4, 0], -1.0, rstd[:, 4 * t:4 * t + 4], ALU.mult, ALU.mult), [rstd_done[t]], "shift")

        def normalise(t, signal):
            for c in range(4 * t, 4 * t + 4):
                a = act.put(lambda e, c=c: e.activation(x[:, c, :], x[:, c, :], ACT.Identity, scale=rstd[:, c:c + 1], bias=shift[:, c:c + 1]), [shift_done[t]], signal)
            return a

        rows_free = [()] * len(rows)
        xn_done, rq_done, expert_in, logits_done, last_scatter = {}, {}, {}, {}, {}

        centered = {}

        def center(t):
            centered[t] = normalise(t, "x1")


        def square_x(t):
            for c in range(4 * t, 4 * t + 4):
                x_squared[t] = sum_squares(x_ss[:, c:c + 1], x[:, c, :], centered[t])

        x_squared, x_rs_done, targets = {}, {}, {}

        def rms_factor(t):
            cut = slice(4 * t, 4 * t + 4)
            x_rs_done[t] = pow_of(x_rs[:, cut], x_ss[:, cut], 1.0 / D, RMS_EPS, [x_squared[t]], "x_rs", keep=x_ms[:, cut])

        def target_rows(t):
            buf = rows[t % 3]
            targets[t] = pool.put(lambda e: e.iota(buf[:, :, :, D:ROW].bitcast(I32).rearrange("p k c o -> p k (c o)"), pattern=[[TOK, TOP_K], [P, 4]], base=4 * t * P, channel_multiplier=1), rows_free[t % 3], "row_targets")

        def feed(t):
            c0, cut, buf, rs = 4 * t, slice(4 * t, 4 * t + 4), rows[t % 3], x_rs_done[t]
            rq_done[t] = dve.put(lambda e: e.tensor_tensor(x_rq[:, cut], x_ms[:, cut], x_rs[:, cut], ALU.mult), [rs], "x_rq")
            for c in range(c0, c0 + 4):
                xn_done[t] = act.put(lambda e, c=c: e.activation(buf[:, 0, c - c0, 0:D], x[:, c, :], ACT.Copy, scale=x_rs[:, c:c + 1]), [rs, *rows_free[t % 3]], "xn")
            a = act.put(lambda e: e.activation(buf[:, 1, :, 0:D], buf[:, 0, :, 0:D], ACT.Copy), [xn_done[t]], "xn")
            last_xn[t] = [a]

        def turn_x(t):
            i, bank, free = act_banks.take()
            for k in range(4):
                m = pe.put(lambda e, k=k: e.transpose(bank[:, k * P:(k + 1) * P], rows[t % 3][:, 0, k, 0:D], ident[:]), [xn_done[t], *free], "xnT")
            a = act.put(lambda e: e.activation(xnT[t], bank[:], ACT.Copy), [m, xT_read[t]], "xnT_copied")
            act_banks.free[i] = (a,)
            rows_free[t % 3] = (m,)
            expert_in[t] = a

        def route(t):
            c0, cut = 4 * t, slice(4 * t, 4 * t + 4)
            i, bank, free = dve_banks.take()
            for k in range(4):
                m = pe.put(lambda e, k=k: e.matmul(bank[:, k * P:(k + 1) * P], xnT[t][:, k * P:(k + 1) * P], router[:], start=True, stop=True), [expert_in[t], router_in, consts, *free], "router")
            routing[t] = (i, bank, m)

        routing, ranking = {}, {}

        def choose(t):
            c0, cut = 4 * t, slice(4 * t, 4 * t + 4)
            i, bank, m = routing[t]
            dl = dve.put(lambda e: e.tensor_tensor(logits[:, cut, :], bank[:].rearrange("p (c r) -> p c r", c=4)[:, :, 0:NR], x_rq[:, cut].unsqueeze(2).to_broadcast([P, 4, NR]), ALU.mult), [m, rq_done[t]], "logits")
            yield
            dve_banks.free[i] = (dl,)
            for c in range(4):
                d = dve.put(lambda e, c=c: e.max(top_v[:, c0 + c, :], logits[:, c0 + c, :]), [dl], "top")
                yield
            for c in range(4):
                d = dve.put(lambda e, c=c: e.max_index(top_i[:, c, :], top_v[:, c0 + c, :], logits[:, c0 + c, :]), [d, row_seen[0]], "top")
                yield
            d = dve.put(lambda e: e.tensor_copy(top_f[:], top_i[:, :, 0:TOP_K]), [d], "top")
            yield
            for k in range(TOP_K):
                d = dve.put(lambda e, k=k: e.tensor_tensor(hot[:, k], expert_no[:].unsqueeze(1).to_broadcast([P, 4, NR]), top_f[:, :, k:k + 1].to_broadcast([P, 4, NR]), ALU.is_equal), [d, consts], "hot")
                yield
            ch = chosen[t % 2]
            logits_done[t] = dve.put(lambda e: e.tensor_tensor(ch[:, 0:4, :], hot[:, 0], hot[:, 1], ALU.add), [d, ranked[0]], "hot")
            yield

        row_seen = [None]
        ranked = [None]
        next_done = [next_row_at]
        row_u_free = [(), ()]

        def rank(t):
            i, bank, free = dve_banks.take()
            ch, n5 = chosen[t % 2], 5 * NR
            pe.put(lambda e: e.matmul(bank[:, 0:n5], before_b[:], ch[:].rearrange("p c r -> p (c r)"), start=True, stop=False, skip_group_check=True), [logits_done[t], c1, *free], "rank")
            for c in range(4):
                m = pe.put(lambda e, c=c: e.matmul(bank[:, (c + 1) * NR:n5].rearrange("p (n r) -> p n r", r=NR), ones_b[:], ch[:, c:c + 1, :].to_broadcast([P, 4 - c, NR]), start=False, stop=(c == 3), skip_group_check=True), [], "rank")
            ranked[0] = m
            ranking[t] = (i, bank, m)

        def rows_to_take(t):
            i, bank, m = ranking[t]
            n5 = 5 * NR
            now, then = next_row[t % 2], next_row[(t + 1) % 2]
            d = dve.put(lambda e: e.tensor_tensor(row_of[:], bank[:, 0:4 * NR].rearrange("p (c r) -> p c r", r=NR), now[:].unsqueeze(1).to_broadcast([P, 4, NR]), ALU.add), [m, next_done[0], row_seen[0]], "rows")
            yield
            dn = dve.put(lambda e: e.tensor_tensor(then[:], bank[:, 4 * NR:n5], now[:], ALU.add), [m, row_seen[0]], "rows")
            yield
            dve_banks.free[i] = (dn,)
            next_done[0] = dn
            for k in range(TOP_K):
                d2 = dve.put(lambda e, k=k: e.tensor_tensor(row_hot[:, k], hot[:, k], row_of[:], ALU.mult), [d, row_seen[0]], "rows")
                yield
            d = dve.put(lambda e: e.tensor_reduce(row_f[:], row_hot[:].rearrange("p k c r -> p (k c) r"), AX.X, ALU.add), [d2], "rows")
            yield
            d = dve.put(lambda e: e.tensor_copy(row_u[t % 2][:], row_f[:]), [d, *row_u_free[t % 2]], "rows")
            yield
            row_seen[0] = d
            row_done[t] = d

        row_done = {}

        def dispatch(t, n0, n1):
            for n in range(n0, n1):
                k, c = divmod(n, 4)
                s = pool.put(lambda e, n=n, k=k, c=c: e.indirect_dma_start(dispatched, bass.IndirectOffsetOnAxis(ap=row_u[t % 2][:, n:n + 1], axis=0), rows[t % 3][:, k, c, :], None),
                             [row_done[t], *last_xn[t], targets[t]], f"dispatched{t % 2}", 16)
            if n1 == 4 * TOP_K:
                rows_free[t % 3] = (*rows_free[t % 3], s)
                row_u_free[t % 2] = (s,)
                last_scatter[t] = s

        hid_free = [()] * len(hid)
        xnT_read = []
        hid_done = {}
        acc_done = {}

        def scale_w1(w1, nos, loaded):
            for n, k in enumerate(nos):
                made = dve.put(lambda e, n=n, k=k: e.tensor_scalar(w1[:, n], w1[:, n], rms_w[:, k:k + 1], None, ALU.mult), [loaded, rms_w_in], "w1_scaled")
            return made

        def shared_hidden(t, u):
            e_no, k = divmod(u, HB)
            h = (4 * t + u) % len(hid)
            i, bank, free = act_banks.take()
            m = pe.put(lambda e: e.matmul(bank[:], w1_shared[:, e_no, k * P:(k + 1) * P], xnT[t], start=True, stop=True),
                       [w1s_ready, expert_in[t], *free], "hidden")
            a = act.put(lambda e: e.activation(hid[h][:], bank[:], ACT.Silu), [m, *hid_free[h]], "hidden_silu")
            act_banks.free[i] = (a,)
            hid_done[t] = a
            xnT_read.append(m)

        def shared_down(t, c):
            n = (NE - NR) * HB
            for u in range(n):
                e_no, k = divmod(u, HB)
                m = pe.put(lambda e, u=u, e_no=e_no, k=k: e.matmul(down_bank[:, c * P:(c + 1) * P], hid[(4 * t + u) % len(hid)][:, c * P:(c + 1) * P], w2_shared[:, e_no, k, :], start=(u == 0), stop=(u == n - 1)),
                           [hid_done[t], w2_in, *bank_free["down"]], "down")
            if c == 3:
                for u in range(n):
                    hid_free[(4 * t + u) % len(hid)] = (m,)
                down_made[t] = m

        down_made = {}

        def add_shared(t):
            acc_done[t] = dve.put(lambda e: e.tensor_tensor(x[:, 4 * t:4 * t + 4, :], down_bank[:].rearrange("p (c d) -> p c d", c=4), x[:, 4 * t:4 * t + 4, :], ALU.add), [down_made[t], *last_xn[t]], "shared_added")
            bank_free["down"] = (acc_done[t],)

        def gate_weights():
            best = top_v[:, :, 0:1]
            d = dve.put(lambda e: e.tensor_tensor(gexp[:], logits[:], best.to_broadcast([P, NC, NR]), ALU.subtract), [logits_done[NT - 1]], "gate")
            d = dve.put(lambda e: e.tensor_tensor(pick_v[:], top_v[:, :, 0:TOP_K], best.to_broadcast([P, NC, TOP_K]), ALU.subtract), [], "gate")
            a = act.put(lambda e: e.activation(gexp[:], gexp[:], ACT.Exp), [d], "gate_exp")
            a = act.put(lambda e: e.activation(pick_v[:], pick_v[:], ACT.Exp), [], "gate_exp")
            d = dve.put(lambda e: e.tensor_reduce(gsum[:], gexp[:], AX.X, ALU.add), [a], "gate")
            d = dve.put(lambda e: e.reciprocal(gsum[:], gsum[:]), [d], "gate")
            d = dve.put(lambda e: e.tensor_tensor(pick_v[:], pick_v[:], gsum[:].unsqueeze(2).to_broadcast([P, NC, TOP_K]), ALU.mult), [d], "gate")
            d = dve.put(lambda e: e.tensor_reduce(gden[:], pick_v[:], AX.X, ALU.add), [d], "gate")
            d = dve.put(lambda e: e.tensor_scalar(gden[:], gden[:], GATE_EPS, None, ALU.add), [d], "gate")
            d = dve.put(lambda e: e.reciprocal(gden[:], gden[:]), [d], "gate")
            return dve.put(lambda e: e.tensor_tensor(pick_v[:], pick_v[:], gden[:].unsqueeze(2).to_broadcast([P, NC, TOP_K]), ALU.mult), [d], "gate")

        TP = SLOT_TILES // 8
        spare = mix[0][:].rearrange("p h i -> p (h i)")
        lower = carve(NR * NR).rearrange("p (a b) -> p a b", a=NR)
        is_past = carve(8 * NR)[0:TP, :].rearrange("p (n r) -> p n r", r=NR)
        is_in = carve(8 * NR)[0:TP, :].rearrange("p (n r) -> p n r", r=NR)
        end_row, tiles_of, tile_base, tile_end, row_base_all = (carve(NR) for _ in range(5))
        row_base = row_base_all[0:TP, :]
        fill_row = sb("fill_row", [P, NR], I32)
        count_i = sb("count_i", [P, NR], I32)
        tile_no = sb("tile_no", [TP, 8])
        tile_no_i = sb("tile_no_i", [TP, 8], I32)
        spare = mix[1][:].rearrange("p h i -> p (h i)")
        in_any, t_expert, t_row = (carve(8)[0:TP, :] for _ in range(3))
        expert_reg = sb("expert_reg", [TP, 8], I32)
        row_reg = sb("row_reg", [TP, 8], I32)

        def tables():
            now = next_row[NT % 2]
            d0 = dve.put(lambda e: e.tensor_copy(fill_row[:], now[:]), [next_done[0]], "table")
            load_regs(sp, ET.SP, "end", fill_row, 0, d0)
            for n in range(NR):
                filled = sp.put(lambda e, n=n: e.dma_start(dispatched[bass.ds(regs["end", n], P), :], filler[:]), [d0], "filled", 16)
            d = dve.put(lambda e: e.scalar_tensor_tensor(end_row[:], expert_no[:], -float(REGION), now[:], ALU.mult, ALU.add), [d0], "table")
            d = dve.put(lambda e: e.tensor_scalar(count_i[:], end_row[:], float(P - 1), None, ALU.add), [d], "table")
            d = dve.put(lambda e: e.tensor_scalar(count_i[:], count_i[:], P.bit_length() - 1, None, ALU.arith_shift_right), [d], "table")
            d = dve.put(lambda e: e.tensor_copy(tiles_of[:], count_i[:]), [d], "table")
            d = dve.put(lambda e: e.tensor_tensor(lower[:], expert_no[:].unsqueeze(1).to_broadcast([P, NR, NR]), expert_no[:].unsqueeze(2).to_broadcast([P, NR, NR]), ALU.is_lt), [d], "table")
            d = dve.put(lambda e: e.tensor_tensor(lower[:], lower[:], tiles_of[:].unsqueeze(1).to_broadcast([P, NR, NR]), ALU.mult), [d], "table")
            d = dve.put(lambda e: e.tensor_reduce(tile_base[:], lower[:], AX.X, ALU.add), [d], "table")
            d = dve.put(lambda e: e.tensor_tensor(tile_end[:], tile_base[:], tiles_of[:], ALU.add), [d], "table")
            d = dve.put(lambda e: e.tensor_scalar(row_base[:], tile_base[0:TP, :], -float(P), None, ALU.mult), [d], "table")
            d = dve.put(lambda e: e.scalar_tensor_tensor(row_base[:], expert_no[0:TP, :], float(REGION), row_base[:], ALU.mult, ALU.add), [d], "table")
            tn = tile_no[:].unsqueeze(2).to_broadcast([TP, 8, NR])
            by_tile = lambda a: a.unsqueeze(1).to_broadcast([TP, 8, NR])
            d = dve.put(lambda e: e.tensor_tensor(is_past[:], tn, by_tile(tile_end[0:TP, :]), ALU.is_ge), [d, tile_no_done], "table")
            d = dve.put(lambda e: e.tensor_tensor(is_in[:], tn, by_tile(tile_base[0:TP, :]), ALU.is_ge), [d], "table")
            d = dve.put(lambda e: e.tensor_tensor(is_in[:], is_in[:], is_past[:], ALU.subtract), [d], "table")
            d = dve.put(lambda e: e.tensor_reduce(in_any[:], is_in[:], AX.X, ALU.add), [d], "table")
            d = dve.put(lambda e: e.tensor_reduce(t_expert[:], is_past[:], AX.X, ALU.add), [d], "table")
            ex = dve.put(lambda e: e.tensor_scalar(expert_reg[:], t_expert[:], float(NR - 1), None, ALU.min), [d], "table")
            d = dve.put(lambda e: e.tensor_tensor(is_in[:], is_in[:], by_tile(row_base[:]), ALU.mult), [ex], "table")
            d = dve.put(lambda e: e.tensor_reduce(t_row[:], is_in[:], AX.X, ALU.add), [d], "table")
            d = dve.put(lambda e: e.scalar_tensor_tensor(t_expert[:], tile_no[:], float(P), in_any[:], ALU.mult, ALU.mult), [d], "table")
            d = dve.put(lambda e: e.tensor_tensor(t_row[:], t_row[:], t_expert[:], ALU.add), [d], "table")
            d = dve.put(lambda e: e.tensor_scalar(in_any[:], in_any[:], -float(NR * REGION), float(NR * REGION), ALU.mult, ALU.add), [d], "table")
            d = dve.put(lambda e: e.tensor_tensor(row_reg[:], t_row[:], in_any[:], ALU.add), [d], "table")
            return filled, ex, d

        regs = {}

        def load_regs(q, engine, name, table, n, after):
            def make(e):
                hi = NR - 1 if name == "expert" else NR * REGION
                width = NR if name == "end" else 8
                _, vals = nc.values_load_multi_w_load_instructions(table[n // 8:n // 8 + 1, 0:width], engines=(engine,), min_val=0, max_val=hi, skip_runtime_bounds_check_because="worked out from counts")
                for j, v in enumerate(vals):
                    regs[q.name if name != "end" else "end", n + j] = v
            q.put(make, [after])

        slots_free = [()] * len(slots_in)
        slots_done = {}
        slotsT_free, slotsT_done = [()] * len(slotsT), {}
        w1_free, w1_done = [()] * len(w1_now), {}
        hr_free, hr_done = [()] * len(hidden_r), {}
        out_free = [()] * len(slots_out)

        def fetch(gr, tab):
            if gr % 2 == 0:
                load_regs(sp, ET.SP, "row", row_reg, 4 * gr, tab[2])
            b = gr % len(slots_in)
            for n in range(4):
                s = sp.put(lambda e, n=n: e.dma_start(slots_in[b][:, n, :], dispatched[bass.ds(regs["sp", 4 * gr + n], P), :]),
                           [*slots_free[b], *slots_ready], f"slots_in{b}", 16)
            slots_done[gr] = s

        def turn_slots(gr):
            b = gr % len(slots_in)
            i, bank, free = dve_banks.take()
            for n in range(4):
                m = pe.put(lambda e, n=n: e.transpose(bank[:, n * P:(n + 1) * P], slots_in[b][:, n, 0:D], ident[:]), [slots_done[gr], *free], "slotsT")
            d = dve.put(lambda e: e.tensor_copy(slotsT[gr % len(slotsT)], bank[:]), [m, xnT_read[AREA_UNITS - 1], *slotsT_free[gr % len(slotsT)]], "slotsT_copied")
            dve_banks.free[i] = (d,)
            slots_free[b] = (m,)
            slotsT_done[gr] = d

        def pick_w1(n, tab):
            if n % 8 == 0:
                load_regs(dve, ET.DVE, "expert", expert_reg, n, tab[1])
            b = n % len(w1_now)
            w1_done[n] = dve.put(lambda e: e.tensor_copy(w1_now[b], w1_routed[:, bass.ds(regs["dve", n], 1), :].rearrange("p o f -> p (o f)")), [w1r_ready[0], xnT_read[AREA_UNITS - 1], *w1_free[b]], "w1_picked")

        def routed_hidden(n2):
            i, bank, free = act_banks.take()
            for n in (2 * n2, 2 * n2 + 1):
                gr, b = n // 4, n % len(w1_now)
                for k in range(HB):
                    at = (n % 2 * HB + k) * P
                    m = pe.put(lambda e, at=at, k=k, b=b, gr=gr, n=n: e.matmul(bank[:, at:at + P], w1_now[b][:, k * P:(k + 1) * P], slotsT[gr % len(slotsT)][:, n % 4 * P:(n % 4 + 1) * P], start=True, stop=True),
                               [w1_done[n], slotsT_done[gr], *free], "routed_hidden")
                w1_free[b] = (m,)
            if n % 4 == 3:
                slotsT_free[gr % len(slotsT)] = (m,)
            hb = n2 % len(hidden_r)
            hr_done[n2] = act.put(lambda e: e.activation(hidden_r[hb], bank[:], ACT.Silu), [m, *hr_free[hb]], "routed_silu")
            act_banks.free[i] = (hr_done[n2],)

        def routed_down(gr, tab):
            if gr % 2 == 0:
                load_regs(pe, ET.PE, "expert", expert_reg, 4 * gr, tab[1])
            i, bank, free = dve_banks.take()
            for n in range(4 * gr, 4 * gr + 4):
                n2, j = n // 2, n % 4
                hb = n2 % len(hidden_r)
                for k in range(HB):
                    at = (n % 2 * HB + k) * P
                    m = pe.put(lambda e, n=n, k=k, at=at, hb=hb, j=j: e.matmul(bank[:, j * P:(j + 1) * P], hidden_r[hb][:, at:at + P], w2_routed[:, bass.ds(regs["pe", n], 1), k * D:(k + 1) * D].rearrange("p o f -> p (o f)"), start=(k == 0), stop=(k == HB - 1)),
                               [hr_done[n2], w2r_in[0], *free], "routed_down")
                hr_free[hb] = (m,)
            b, sb_ = gr % len(slots_out), gr % len(slots_in)
            d = dve.put(lambda e: e.tensor_copy(slots_out[b], bank[:]), [m, *out_free[b]], "routed_out")
            dve_banks.free[i] = (d,)
            for n in range(4):
                s = pool.put(lambda e, n=n: e.indirect_dma_start(returned, bass.IndirectOffsetOnAxis(ap=slots_in[sb_][:, n, D:ROW].bitcast(U32), axis=0), slots_out[b][:, n * P:(n + 1) * P], None, bounds_check=NOWHERE - 1, oob_is_err=False),
                             [d], f"returned{b}", 16)
            out_free[b] = (s,)
            slots_free[sb_] = (*slots_free[sb_], s)
            return s

        picked_free = [()] * len(picked)
        picked_done = {}

        def gather(t, done):
            b = t % len(picked)
            for k in range(TOP_K):
                src = returned[k * TOK + t * W:k * TOK + (t + 1) * W, :].rearrange("(c p) d -> p c d", p=P)
                s = sp.put(lambda e, k=k, src=src: e.dma_start(picked[b][:, k], src), [*done, *picked_free[b]], f"picked{b}", 16)
            picked_done[t] = s

        scaled_done = {}

        def scale_second(t, gate):
            b = t % len(picked)
            for c in range(4 * t, 4 * t + 4):
                scaled_done[t] = act.put(lambda e, c=c: e.activation(picked[b][:, 1, c % 4, :], picked[b][:, 1, c % 4, :], ACT.Copy, scale=pick_v[:, c, 1:2]), [picked_done[t], gate], "second_scaled")

        def finish(t, gate):
            b = t % len(picked)
            for c in range(4 * t, 4 * t + 4):
                d = dve.put(lambda e, c=c: e.scalar_tensor_tensor(x[:, c, :], picked[b][:, 0, c % 4, :], pick_v[:, c, 0:1], x[:, c, :], ALU.mult, ALU.add),
                            [picked_done[t], gate, acc_done[t]], "routed_added")
                yield
            d = dve.put(lambda e: e.tensor_tensor(x[:, 4 * t:4 * t + 4, :], x[:, 4 * t:4 * t + 4, :], picked[b][:, 1], ALU.add), [d, scaled_done[t]], "routed_added")
            yield
            picked_free[b] = (d,)
            yield from ln_stats(t, d)
            rstd_done[t] = pow_of(rstd[:, 4 * t:4 * t + 4], mv[:, 4 * t:4 * t + 4, 1], 1.0, LN_EPS, [stats[t]], "rstd")

        def store(t):
            a = normalise(t, "x2")
            return sp.put(lambda e: e.dma_start(out_d[:, 4 * t:4 * t + 4, :], x[:, 4 * t:4 * t + 4, :]), [a], "stored", 16)

        tile_no_done = pool.put(lambda e: e.iota(tile_no_i[:], pattern=[[1, 8]], base=0, channel_multiplier=8), [], "consts")
        tile_no_done = pool.put(lambda e: e.tensor_copy(tile_no[:], tile_no_i[:]), [tile_no_done], "consts")
        dec, zt, gated = {}, {}, {}
        head = steps_of(0, CPB)
        while 0 not in log_decays_done:
            next(head)
        for c in range(4):
            arows_of(c)
        w1r_ready, w2r_in, last_xn = [None], [None], {}
        AHEAD = 5

        LAG = 32
        DRAIN = NC + 4
        later = iter(())

        def shared_units(i):
            past = lambda i: max(0, i - LAG) if i < DRAIN else DRAIN - LAG + 2 * (i - DRAIN)
            return [u for u in range(past(i), past(i + 1)) if u < NC + 4]

        def interleave(chains):
            while chains:
                chains = [g for g in chains if next(g, g) is not g]
                next(later, None)

        def at(i, lo, n):
            return 0 <= i - lo < n
        for i in range(-AHEAD, NC + 32):
            def due(n, work):
                t = (i - n) // 4
                if (i - n) % 4 == 0 and 0 <= t < NT:
                    work(t)
            if i == -2:
                interleave([head])
                for n in range(4):
                    dec[n] = decays_of(n)
            if i == -3:
                later = steps_of(CPB, 2 * CPB)
            if i == 3:
                later = steps_of(2 * CPB, NC)
            if i in (1, 9):
                interleave([later])
            if i == 8:
                w1s_ready = scale_w1(w1_shared, range(NR, NE), w1_in)
            if at(i, 1, NC):
                zt[i - 1] = z_of(i - 1)
            if at(i, 0, NC):
                turn_xb(i)
            if 0 <= i + AHEAD - 2 < NT * NBLK:
                conv_silu(i + AHEAD - 2)
            if 0 <= i + AHEAD < NT * NBLK:
                conv_project(i + AHEAD)
            if at(i, 4, NC):
                turn_g(i - 4)
            for u in shared_units(i):
                if 4 <= u:
                    shared_down((u - 4) // 4, u % 4)
                if u < NC:
                    shared_hidden(u // 4, u % 4)
            if at(i, 5, NC):
                project(i - 5)
            if i % 4 == 2 and 4 <= i + 2 < NC:
                for n in range(i + 2, i + 6):
                    dec[n] = decays_of(n)
            due(12, center)
            due(12, square_x)
            due(15, feed)
            due(16, turn_x)
            due(17, route)
            due(19, rank)
            due(8, g_factor)
            due(10, ln_factor)
            due(13, rms_factor)
            due(15, target_rows)
            if 4 <= i + 7 < NC:
                arows_of(i + 7)
            chains = []
            if at(i, 3, NC):
                next_state(i - 3)
            if at(i, 2, NC):
                keep_state(i - 2)
            if 0 <= i + AHEAD - 1 < NT * NBLK:
                chains.append(conv_taps(i + AHEAD - 1))
            if at(i, 1, NC):
                chains.append(gram_then_mix(i - 1))
                chains.append(scale_x(i - 1))
            if at(i, 3, NC):
                chains.append(gate_y(i - 3))
            due(18, lambda t: chains.append(choose(t)))
            due(20, lambda t: chains.append(rows_to_take(t)))
            interleave(chains)
            if i == 4 * (NT - 1) + 20:
                tab = tables()
            due(8, lambda t: interleave([residual(t)]))
            for n in range(4):
                due(21 + n, lambda t: t < NT - 1 and dispatch(t, 2 * n, 2 * n + 2))
            for n in range(2):
                due(21 + n, lambda t: t == NT - 1 and dispatch(t, 4 * n, 4 * n + 4))
            if at(i, 0, NC + 2):
                gram_and_state_add(i, i - 2)
            if at(i, 2, NC):
                skip_x(i - 2)
                outputs(i - 2)
            due(11, ln_shift)
            for u in shared_units(i):
                if u >= 4 and u % 4 == 3:
                    add_shared((u - 4) // 4)
            if i == NC + 3:
                w2r_in[0] = sp.put(lambda e: e.dma_start(w2_routed, w2_d[:, 0:NR * HB * D].rearrange("p (e f) -> p e f", e=NR)), [xbc_read[t, n] for n in range(NBLK) for t in (NT - 2, NT - 1)], "w2r_loaded", 16)
                w1r_in = sp.put(lambda e: e.dma_start(w1_routed, w1_v[:, 0:NR]), decay_free, "w1r_loaded", 16)
            if i == NC + 12:
                w1r_ready[0] = scale_w1(w1_routed, range(NR), w1r_in)
        slots_ready = (last_scatter[NT - 1], last_scatter[NT - 2], tab[0], filler_region)
        gate = gate_weights()
        FETCH_AHEAD = len(slots_in) - 1
        for gr in range(FETCH_AHEAD):
            fetch(gr, tab)
        for gr in range(2):
            turn_slots(gr)
            for n in range(4 * gr, 4 * gr + 4):
                pick_w1(n, tab)
        routed_hidden(0)
        routed_hidden(1)
        tails = {}
        for gr in range(GROUPS):
            if gr + 2 < GROUPS:
                turn_slots(gr + 2)
            if gr + 1 < GROUPS:
                routed_hidden(2 * gr + 2)
                routed_hidden(2 * gr + 3)
            if gr + 2 < GROUPS:
                for n in range(4):
                    pick_w1(4 * (gr + 2) + n, tab)
            tails[gr % len(slots_out)] = routed_down(gr, tab)
            if gr + FETCH_AHEAD < GROUPS:
                fetch(gr + FETCH_AHEAD, tab)
        done = list(tails.values())
        for t in range(NT + 3):
            if t == 0:
                for n in range(len(picked)):
                    gather(n, done)
                scale_second(0, gate)
            if t + 1 < NT:
                scale_second(t + 1, gate)
            if t < NT:
                interleave([finish(t, gate)])
                if t + len(picked) < NT:
                    gather(t + len(picked), done)
            if 0 <= t - 1 < NT:
                ln_shift(t - 1)
            if 0 <= t - 2 < NT:
                last = store(t - 2)
        sp.put(lambda e: e.nop(), [last])

        semaphores = {n: ctx.enter_context(nc.semaphore(n)) for n in counts}
        block = ctx.enter_context(nc.Block())

        @block.sync
        def _(e):
            sp.play(e, semaphores)

        @block.scalar
        def _(e):
            act.play(e, semaphores)

        @block.vector
        def _(e):
            dve.play(e, semaphores)

        @block.gpsimd
        def _(e):
            pool.play(e, semaphores)

        @block.tensor
        def _(e):
            pe.play(e, semaphores)


def kernel(**inputs):
    import numpy as np
    import concourse.bacc as bacc
    from concourse.bass_utils import run_bass_kernel_spmd

    a = {n: np.asarray(v) for n, v in inputs.items()}
    x = a["L0_attn_x"]
    nb, length, d = x.shape
    tokens = x.reshape(nb * length, d)
    chunks = tokens.shape[0] // P

    def channels(v, n=P):
        return np.moveaxis(v.reshape(*v.shape[:-1], -1, n), -1, 0)

    def rows(v):
        return np.broadcast_to(v[None], (P, *v.shape))

    w1 = np.concatenate([a["L0_ffn_w1"], a["L0_ffn_w1_s"]])
    w2 = np.concatenate([a["L0_ffn_w2"], a["L0_ffn_w2_s"]])
    rms = np.concatenate([a["L0_ffn_rms_w"], a["L0_ffn_rms_w_s"]])
    arrays = {
        "xT": tokens.T,
        "x": tokens.reshape(chunks, P, d).transpose(1, 0, 2),
        "w_in": a["L0_attn_in_proj_w"],
        "conv_w": channels(a["L0_attn_conv_w"]).transpose(0, 2, 1),
        "conv_b": channels(a["L0_attn_conv_b"]),
        "norm_w": channels(a["L0_attn_norm_w"]),
        "w_out": a["L0_attn_out_proj_w"].reshape(-1, P, d).transpose(1, 0, 2),
        "dt_bias": rows(a["L0_attn_dt_bias"]),
        "a_log": rows(a["L0_attn_A_log"]),
        "d_skip": rows(a["L0_attn_D"]),
        "router": a["L0_ffn_router_w"],
        "rms_w": rms.T,
        "w1": w1.transpose(1, 0, 2).reshape(d, -1),
        "w2": w2.reshape(w2.shape[0], -1, P, d).transpose(2, 0, 1, 3).reshape(P, -1),
    }
    arrays = {n: np.ascontiguousarray(v) for n, v in arrays.items()}
    nc = bacc.Bacc("TRN2", target_bir_lowering=False, num_devices=1)
    args = [nc.dram_tensor(n + "_dram", v.shape, F32, kind="ExternalInput").ap() for n, v in arrays.items()]
    out = nc.dram_tensor("out_dram", (P, chunks, d), F32, kind="ExternalOutput").ap()
    mamba_moe(nc, *args, out)
    r = run_bass_kernel_spmd(nc, [{n + "_dram": v for n, v in arrays.items()}], core_ids=[0])
    got = r.results[0]["out_dram"]
    return np.ascontiguousarray(got.transpose(1, 0, 2)).reshape(nb, length, d)
```
